# Optimizing a Trainium2 kernel written in Bass

```python
import numpy as np
import jax
import jax.numpy as jnp

def _softmax(x, axis=-1):
    return jax.nn.softmax(x, axis=axis)

def _gelu(x):
    return jax.nn.gelu(x, approximate=True)

def _silu(x):
    return jax.nn.silu(x)

def _sigmoid(x):
    return jax.nn.sigmoid(x)

def _layernorm(x, axis=-1, eps=1e-05):
    m = jnp.mean(x, axis=axis, keepdims=True)
    v = jnp.var(x, axis=axis, keepdims=True)
    return (x - m) / jnp.sqrt(v + eps)

def _scatter_add(tgt, idx, src, axis=0):
    return tgt.at[idx].add(src)

def _segment_sum(src, seg, n):
    return jax.ops.segment_sum(src, seg, n)
kernel_name = 'mk_xattn_ffn_d2_seqx_r8_1b7051'

def setup_inputs(seed: int=0):
    np.random.seed(seed)
    _w = jnp.asarray

    def _rec_inputs():
        import jax
        import jax.numpy as jnp
        _rk = jax.random.key(seed)
        x = 7.22e-05 + 1 * jax.random.normal(jax.random.fold_in(_rk, 1), (4, 512, 128), jnp.float32)
        _lenS = 512 - jax.random.randint(jax.random.fold_in(_rk, 7), (4,), 0, max(1, 512 // 4) + 1, jnp.int32)
        _lenS2 = 32 - jax.random.randint(jax.random.fold_in(_rk, 8), (4,), 0, max(1, 32 // 4) + 1, jnp.int32)
        _ctx_1024P = jax.random.normal(jax.random.fold_in(_rk, 11), (4, 16, 128), jnp.float32)
        _ctx_1024c = jax.random.dirichlet(jax.random.fold_in(_rk, 511), 0.3 * jnp.ones((16,), jnp.float32), (4, 32))
        _ctx_1024t = jnp.einsum('bsk,bkd->bsd', _ctx_1024c, _ctx_1024P)
        _ctx_1024t = _ctx_1024t * jax.lax.rsqrt(jnp.mean(jnp.square(_ctx_1024t)) + 1e-12) * 0.953939
        ctx_1024 = 4.13588e-05 + 0.999923 * (_ctx_1024t + 0.3 * jax.random.normal(jax.random.fold_in(_rk, 611), (4, 32, 128), jnp.float32))
        return (x, ctx_1024)
    x, ctx_1024 = _rec_inputs()

    def _L0_xattn_setup():
        import jax, jax.numpy as jnp
        import numpy as np
        D_MODEL = 128
        NUM_HEADS = 16
        D_K = D_MODEL // NUM_HEADS
        key = jax.random.key(seed)
        ks = jax.random.split(key, 11)
        B, S = (4, 256)
        s = 1.0 / np.sqrt(D_MODEL)
        inp = {'q': jax.random.normal(ks[0], (B, S, D_MODEL), jnp.float32), 'k': jax.random.normal(ks[1], (B, S, D_MODEL), jnp.float32), 'v': jax.random.normal(ks[2], (B, S, D_MODEL), jnp.float32), 'Wq': jax.random.normal(ks[3], (D_MODEL, D_MODEL), jnp.float32) * s, 'bq': jnp.zeros((D_MODEL,), jnp.float32), 'Wk': jax.random.normal(ks[4], (D_MODEL, D_MODEL), jnp.float32) * s, 'bk': jnp.zeros((D_MODEL,), jnp.float32), 'Wv': jax.random.normal(ks[5], (D_MODEL, D_MODEL), jnp.float32) * s, 'bv': jnp.zeros((D_MODEL,), jnp.float32), 'Wo': jax.random.normal(ks[6], (D_MODEL, D_MODEL), jnp.float32) * s, 'bo': jnp.zeros((D_MODEL,), jnp.float32)}
        return inp
    _L0_xattn_all = _L0_xattn_setup()
    _L0_xattn_in = {k: v for k, v in _L0_xattn_all.items() if k in ('Wq', 'bq', 'Wk', 'bk', 'Wv', 'bv', 'Wo', 'bo')}
    del _L0_xattn_all

    def _L0_ffn_setup():
        import jax, jax.numpy as jnp
        import numpy as np
        B, S, D = (4, 256, 128)
        O = 128
        E = 8
        K = 2
        key = jax.random.key(seed)
        k1, k2, k3, k4, k5 = jax.random.split(key, 5)
        scale = 1.0 / np.sqrt(D)
        x = jax.random.normal(k1, (B, S, D), dtype=jnp.float32)
        We = jax.random.uniform(k2, (E, D, O), dtype=jnp.float32, minval=-scale, maxval=scale)
        be = jax.random.uniform(k3, (E, O), dtype=jnp.float32, minval=-scale, maxval=scale)
        Wg = jax.random.uniform(k4, (D, E), dtype=jnp.float32, minval=-scale, maxval=scale)
        bg = jax.random.uniform(k5, (E,), dtype=jnp.float32, minval=-scale, maxval=scale)
        return {'x': x, 'We': We, 'be': be, 'Wg': Wg, 'bg': bg}
    _L0_ffn_all = _L0_ffn_setup()
    _L0_ffn_in = {k: v for k, v in _L0_ffn_all.items() if k in ('We', 'be', 'Wg', 'bg')}
    del _L0_ffn_all

    def _L1_xattn_setup():
        import jax, jax.numpy as jnp
        import numpy as np
        from jax import lax
        B, T, F = (32, 128, 128)
        CONV_UNITS = 256
        SHORT_UNITS = 256
        RATE = 4
        key = jax.random.key(seed)
        k1, k2, k3 = jax.random.split(key, 3)
        inputs = jax.random.normal(k1, (B, T, F), dtype=jnp.float32)
        memory = jax.random.normal(k2, (B, CONV_UNITS + SHORT_UNITS, F), dtype=jnp.float32)
        conv_w = jax.random.normal(k3, (RATE, F, F), dtype=jnp.float32) * 0.02
        conv_b = jnp.zeros((F,), dtype=jnp.float32)
        return {'inputs': inputs, 'memory': memory, 'conv_w': conv_w, 'conv_b': conv_b, 'conv_units': CONV_UNITS, 'short_units': SHORT_UNITS, 'rate': RATE}
    _L1_xattn_all = _L1_xattn_setup()
    _L1_xattn_in = {k: v for k, v in _L1_xattn_all.items() if k in ('conv_w', 'conv_b')}
    del _L1_xattn_all

    def _L1_ffn_setup():
        import jax, jax.numpy as jnp
        import numpy as np
        B, S, D = (4, 256, 128)
        E, K = (8, 2)
        H = 176
        key = jax.random.key(seed)
        kx, kr, k1, k2, k3 = jax.random.split(key, 5)
        s = 0.02
        return {'x': jax.random.normal(kx, (B, S, D), dtype=jnp.float32), 'w_router': jax.random.normal(kr, (E, D), dtype=jnp.float32) * s, 'w1': jax.random.normal(k1, (E, D, H), dtype=jnp.float32) * s, 'w2': jax.random.normal(k2, (E, H, D), dtype=jnp.float32) * s, 'w3': jax.random.normal(k3, (E, D, H), dtype=jnp.float32) * s}
    _L1_ffn_all = _L1_ffn_setup()
    _L1_ffn_in = {k: v for k, v in _L1_ffn_all.items() if k in ('w_router', 'w1', 'w2', 'w3')}
    del _L1_ffn_all
    return {'x': x, 'ctx_1024': ctx_1024, 'L0_xattn_Wq': _L0_xattn_in['Wq'], 'L0_xattn_bq': _L0_xattn_in['bq'], 'L0_xattn_Wk': _L0_xattn_in['Wk'], 'L0_xattn_bk': _L0_xattn_in['bk'], 'L0_xattn_Wv': _L0_xattn_in['Wv'], 'L0_xattn_bv': _L0_xattn_in['bv'], 'L0_xattn_Wo': _L0_xattn_in['Wo'], 'L0_xattn_bo': _L0_xattn_in['bo'], 'L0_ffn_We': _L0_ffn_in['We'], 'L0_ffn_be': _L0_ffn_in['be'], 'L0_ffn_Wg': _L0_ffn_in['Wg'], 'L0_ffn_bg': _L0_ffn_in['bg'], 'L1_xattn_conv_w': _L1_xattn_in['conv_w'], 'L1_xattn_conv_b': _L1_xattn_in['conv_b'], 'L1_ffn_w_router': _L1_ffn_in['w_router'], 'L1_ffn_w1': _L1_ffn_in['w1'], 'L1_ffn_w2': _L1_ffn_in['w2'], 'L1_ffn_w3': _L1_ffn_in['w3']}

def reference(x, ctx_1024, L0_xattn_Wq, L0_xattn_bq, L0_xattn_Wk, L0_xattn_bk, L0_xattn_Wv, L0_xattn_bv, L0_xattn_Wo, L0_xattn_bo, L0_ffn_We, L0_ffn_be, L0_ffn_Wg, L0_ffn_bg, L1_xattn_conv_w, L1_xattn_conv_b, L1_ffn_w_router, L1_ffn_w1, L1_ffn_w2, L1_ffn_w3):
    import jax
    import jax.numpy as jnp

    def _L0_xattn_ref(q, k, v, Wq, bq, Wk, bk, Wv, bv, Wo, bo):
        import jax, jax.numpy as jnp
        import numpy as np
        D_MODEL = 128
        NUM_HEADS = 16
        D_K = D_MODEL // NUM_HEADS
        B, S, _ = q.shape

        def split_heads(x):
            return x.reshape(B, -1, NUM_HEADS, D_K).transpose(0, 2, 1, 3)
        Q = split_heads(q @ Wq + bq)
        K = split_heads(k @ Wk + bk)
        V = split_heads(v @ Wv + bv)
        scores = jnp.einsum('bhqd,bhkd->bhqk', Q, K) / jnp.sqrt(jnp.float32(D_K))
        attn = jax.nn.softmax(scores, axis=-1)
        out = jnp.einsum('bhqk,bhkd->bhqd', attn, V)
        out = out.transpose(0, 2, 1, 3).reshape(B, -1, D_MODEL)
        return out @ Wo + bo

    def _L0_ffn_ref(x, We, be, Wg, bg):
        import jax, jax.numpy as jnp
        import numpy as np
        B, S, D = (4, 256, 128)
        O = 128
        E = 8
        K = 2
        b, s, d = x.shape
        x_flat = x.reshape(-1, d)
        gates = jax.nn.softmax(x_flat @ Wg + bg, axis=-1)
        topk_gates, topk_idx = jax.lax.top_k(gates, K)
        topk_gates = topk_gates / jnp.sum(topk_gates, axis=1, keepdims=True)
        expert_out = jnp.einsum('nd,edo->neo', x_flat, We) + be
        selected = jnp.take_along_axis(expert_out, topk_idx[:, :, None], axis=1)
        out = jnp.sum(selected * topk_gates[:, :, None], axis=1)
        return out.reshape(b, s, -1)

    def _L1_xattn_ref(inputs, memory, conv_w, conv_b, conv_units, short_units, rate):
        import jax, jax.numpy as jnp
        import numpy as np
        from jax import lax
        B, T, F = (32, 128, 128)
        CONV_UNITS = 256
        SHORT_UNITS = 256
        RATE = 4
        b, t, f = inputs.shape
        conv_mem = memory[:, :conv_units]
        short_mem = memory[:, -short_units:]
        old_memory = short_mem[:, :t]
        compression = lax.conv_general_dilated(old_memory, conv_w, window_strides=(rate,), padding='VALID', dimension_numbers=('NWC', 'WIO', 'NWC')) + conv_b
        tc = compression.shape[1]
        new_short = jnp.concatenate([short_mem[:, t:], inputs], axis=1)
        new_conv = jnp.concatenate([conv_mem[:, tc:], compression], axis=1)
        return jnp.concatenate([new_conv, new_short], axis=1)

    def _L1_ffn_ref(x, w_router, w1, w2, w3):
        import jax, jax.numpy as jnp
        import numpy as np
        B, S, D = (4, 256, 128)
        E, K = (8, 2)
        H = 176
        bsz, seqlen, dim = x.shape
        xf = x.reshape(-1, dim)
        scores = jax.nn.softmax(xf @ w_router.T, axis=-1)
        expert_weights, expert_indices = jax.lax.top_k(scores, K)
        h = jax.nn.silu(jnp.einsum('td,edh->eth', xf, w1)) * jnp.einsum('td,edh->eth', xf, w3)
        y = jnp.einsum('eth,ehd->etd', h, w2)
        y_t = jnp.swapaxes(y, 0, 1)
        sel = jnp.take_along_axis(y_t, expert_indices[:, :, None], axis=1)
        out = jnp.sum(expert_weights[:, :, None] * sel, axis=1)
        return out.reshape(bsz, seqlen, dim)
    x = x + _L0_xattn_ref(_layernorm(x, axis=-1), ctx_1024, ctx_1024, L0_xattn_Wq, L0_xattn_bq, L0_xattn_Wk, L0_xattn_bk, L0_xattn_Wv, L0_xattn_bv, L0_xattn_Wo, L0_xattn_bo)
    x = x + _L0_ffn_ref(_layernorm(x, axis=-1), L0_ffn_We, L0_ffn_be, L0_ffn_Wg, L0_ffn_bg)
    x = x + _L1_xattn_ref(ctx_1024, _layernorm(x, axis=-1), L1_xattn_conv_w, L1_xattn_conv_b, 256, 256, 4)
    x = x + _L1_ffn_ref(_layernorm(x, axis=-1), L1_ffn_w_router, L1_ffn_w1, L1_ffn_w2, L1_ffn_w3)
    return x

_drawn_inputs = setup_inputs


def setup_inputs(seed=0):
    import zlib

    import numpy as np

    out = dict(_drawn_inputs(seed))
    spreads = {'L0_xattn_bq': (0.0, 0.1),
     'L0_xattn_bk': (0.0, 0.8),
     'L0_xattn_bv': (0.0, 0.1),
     'L0_xattn_bo': (0.0, 0.1),
     'L1_xattn_conv_b': (0.0, 0.8)}
    factors = {'L1_ffn_w_router': 8.0, 'L1_ffn_w1': 8.0, 'L1_ffn_w2': 8.0, 'L1_ffn_w3': 8.0}
    for name, (base, spread) in spreads.items():
        noise = np.random.default_rng([zlib.crc32(name.encode()), seed]).standard_normal(out[name].shape)
        drawn = base * np.exp(spread * noise) if base else spread * noise
        out[name] = jnp.asarray(drawn.astype(out[name].dtype))
    for name, factor in factors.items():
        out[name] = (out[name] * factor).astype(out[name].dtype)
    return out
```

```python
import concourse.bass as bass
from concourse import mybir
from contextlib import ExitStack



def order_of_steps(batches, chunks):
    prep = ["stats0", "norm0", "T0", "Q", "M0", "M1", "M2", "M3", "negmaxT", "E0", "E1", "E2", "E3", "V",
            "attnT", "O", "stats1", "norm1", "T1", "route0", "X0", "X1", "X2", "X3", "stats2", "norm2",
            "memory", "stats3", "norm3", "T3", "route1", "gateT"]
    steps = [(s, b) for pair in zip(*([(s, b) for s in prep] for b in (0, 1))) for s, b in pair]
    steps.insert(steps.index(("Q", 1)) + 1, ("first_weights", 0))
    steps.insert(steps.index(("O", 1)) + 1, ("second_weights", 0))
    for b in range(batches):
        hidden = [(f"H{c}", b) for c in range(chunks)]
        ahead = [(s, b + 2) for s in prep] if b + 2 < batches else []
        per = -(-len(ahead) // chunks)
        for c in range(chunks):
            steps.append(hidden[c])
            steps += ahead[c * per:(c + 1) * per]
        steps.append(("out", b))
    return steps


def block_program(nc, x, ctx_1024, Wq, bq, Wk, bk, Wv, bv, Wo, bo, We, be, Wg, bg, conv_w, conv_b,
                  w_router, w1, w2, w3, out):
    f32 = mybir.dt.float32
    f32r = mybir.dt.float32r
    ALU = mybir.AluOpType
    ACT = mybir.ActivationFunctionType
    AX = mybir.AxisListType

    B, S, D = x.shape
    NKEY = ctx_1024.shape[1]
    H = 16
    DK = D // H
    E = We.shape[0]
    HID = w1.shape[2]
    P = 128
    J = S // P
    NC4 = H * NKEY // P
    H4 = H // NC4
    EH = E * HID
    NCH = EH // P
    KC = P // NC4
    VW = DK + 1
    CONV = conv_w.shape[0]
    HALF = S // 2
    COMP = NKEY // CONV
    EPS = 1e-5
    SCALE = float(DK) ** -0.5
    LNS = 4
    assert CONV == J and D == P and NC4 * KC == P

    steps = order_of_steps(B, NCH)

    NSHARED = 3
    uses = {"T0": 1, "Q": 1, "M0": 1, "M1": 1, "M2": 1, "M3": 1, "negmaxT": 1, "E0": 1, "E1": 1, "E2": 1, "E3": 1,
            "V": 2, "attnT": 1, "O": 1, "T1": 1, "route0": 1, "X0": 2, "X1": 2, "X2": 2, "X3": 2, "memory": 2,
            "T3": 1, "route1": 1, "gateT": 1, "out": 1, "first_weights": 1}
    SETUP_USES = 3
    bank_of = {("setup", 0, i): i % NSHARED for i in range(SETUP_USES)}
    n = SETUP_USES
    for s, b in steps:
        for i in range(uses.get(s, 0)):
            bank_of[(s, b, i)] = n % NSHARED
            n += 1

    turn = {}
    for kind in "MEX":
        for i, step in enumerate([step for step in steps if step[0][0] == kind]):
            turn[step] = i + 1

    es = ExitStack()
    with es:
        def sb(name, shape, dt=f32):
            return es.enter_context(nc.sbuf_tensor(name, shape, dt))

        def sem(name):
            return es.enter_context(nc.semaphore(name))

        ident = sb("ident", [P, P])
        ones = sb("ones", [P, P])
        minus_half = sb("minus_half", [P, J])
        rank_desc = sb("rank_desc", [P, J, E])
        head_mask = sb("head_mask", [P, H])
        key_head_mask = sb("key_head_mask", [P, H4])
        head_rows = sb("head_rows", [P, H, NKEY], f32r)
        expert_mask = sb("expert_mask", [P, E])
        expert_rows = sb("expert_rows", [P, E, HID], f32r)
        ones_r = sb("ones_r", [P, P], f32r)

        ctx_sb = sb("ctx_sb", [P, D])
        ctxT = sb("ctxT", [P, B, H4, NKEY])
        Wk_sb = sb("Wk_sb", [P, D])
        Wv_sb = sb("Wv_sb", [P, D])
        Wq_sb = sb("Wq_sb", [P, D])
        Wo_sb = sb("Wo_sb", [P, D])
        bk_col = sb("bk_col", [P, 1])
        bq_col = sb("bq_col", [P, 1])
        bv_row = sb("bv_row", [P, D])
        bo_all = sb("bo_all", [P, D])
        bg_all = sb("bg_all", [P, E])
        convb_all = sb("convb_all", [COMP, D])
        We_sb = sb("We_sb", [P, E, D])
        Wg_sb = sb("Wg_sb", [P, E])
        be_sb = sb("be_sb", [1, E * D])
        conv_sb = sb("conv_sb", [P, CONV, D])
        wr_sb = sb("wr_sb", [E, D])
        w1_sb = sb("w1_sb", [P, E, HID])
        w3_sb = sb("w3_sb", [P, E, HID])
        w2_sb = sb("w2_sb", [P, NCH, D])
        Wq_p = [sb(f"Wq_{s}", [P, D], f32r) for s in ("hi", "lo")]
        Wo_p = [sb(f"Wo_{s}", [P, D], f32r) for s in ("hi", "lo")]
        Wg_p = [sb(f"Wg_{s}", [P, E], f32r) for s in ("hi", "lo")]
        wr_p = [sb(f"wr_{s}", [P, E], f32r) for s in ("hi", "lo")]
        We_p = [sb(f"We_{s}", [P, E * D], f32r) for s in ("hi", "lo")]
        w1_p = [sb(f"w1_{s}", [P, EH], f32r) for s in ("hi", "lo")]
        w3_p = [sb(f"w3_{s}", [P, EH], f32r) for s in ("hi", "lo")]
        be_hilo = sb("be_hilo", [P, E * D], f32r)
        be_lo = sb("be_lo", [1, E * D], f32r)
        KT = sb("KT", [P, B, NKEY])
        KT_p = [sb(f"KT_{s}", [P, B, NKEY], f32r) for s in ("hi", "lo")]
        K_all = [sb(f"K_all_{s}", [P, 2, H, NKEY], f32r) for s in ("hi", "lo")]
        V_aug = sb("V_aug", [P, B, NC4, H4, VW])

        resid = sb("resid", [P, B, J, D])
        memory_rows = sb("memory_rows", [P, B, J * D])
        bn = sb("bn", [P, LNS * B, J, 6])
        mean_var = sb("mean_var", [P, LNS * B, J, 2])
        var_eps = sb("var_eps", [P, LNS * B, J])
        rstd = sb("rstd", [P, LNS * B, J])
        xn = sb("xn", [P, 2, J, D])
        xT_p = [sb(f"xT_{s}", [P, 2, S], f32r) for s in ("hi", "lo")]
        x4T_p = [sb(f"x4T_{s}", [P, 3, S], f32r) for s in ("hi", "lo")]
        q_p = [sb(f"q_{s}", [P, 2, S], f32r) for s in ("hi", "lo")]
        negmax = sb("negmax", [P, 2, J, H])
        negmaxT = sb("negmaxT", [P, 2, S], f32r)
        probsT = sb("probsT", [P, 2, NC4, S])
        rden = sb("rden", [P, 2, 2 * H])
        attn = sb("attn", [P, 2, J, H, DK])
        aT_p = [sb(f"aT_{s}", [P, 2, S], f32r) for s in ("hi", "lo")]
        rt = [[sb(f"rt{k}_{i}", [P, J, E]) for i in range(9)] for k in range(2)]
        rs = [[sb(f"rs{k}_{i}", [P, J]) for i in range(6)] for k in range(2)]
        gate = sb("gate", [P, 2, B, J, E])
        gate_hilo = sb("gate_hilo", [P, B, J, 2 * E], f32r)
        gateT = sb("gateT", [P, 3, S], f32r)
        convT = sb("convT", [P, J, COMP])
        comp = sb("comp", [COMP, D])
        silu_h = sb("silu_h", [P, 2, S])
        gate_bc = sb("gate_bc", [P, 2, S])
        gated = sb("gated", [P, 2, S])
        hidden = sb("hidden", [P, 2, S])
        yT = We_sb[:, 0:J, :].rearrange("p e o -> p (e o)")

        bank = [es.enter_context(nc.psum_tensor(f"bank{i}", [P, S], f32)) for i in range(NSHARED)]
        ps_h1 = es.enter_context(nc.psum_tensor("ps_h1", [P, S], f32))
        ps_h3 = [es.enter_context(nc.psum_tensor(f"ps_h3{i}", [P, S], f32)) for i in range(2)]
        ps_gate = es.enter_context(nc.psum_tensor("ps_gate", [P, S], f32))
        ps_y = es.enter_context(nc.psum_tensor("ps_y", [P, S], f32))

        ld_ctx, ld_q, ld_ffn0, ld_conv, ld_w13, ld_w2 = (sem(s) for s in (
            "ld_ctx", "ld_q", "ld_ffn0", "ld_conv", "ld_w13", "ld_w2"))
        ld_x = [sem(f"ld_x{b}") for b in range(B)]
        be_moved = sem("be_moved")
        consts_ready, zeros_ready, masks_ready = sem("consts_ready"), sem("zeros_ready"), sem("masks_ready")
        ctxT_psum, ctxT_ready, kv_psum, KT_ready, KT_hi, KT_lo, K_all_ready, V_ready = (sem(s) for s in (
            "ctxT_psum", "ctxT_ready", "kv_psum", "KT_ready", "KT_hi_s", "KT_lo_s", "K_all_ready", "V_ready"))
        wr_psum, wr_hi, wr_lo = sem("wr_psum"), sem("wr_hi"), sem("wr_lo")
        W_hi, W_lo, be_ready = sem("W_hi"), sem("W_lo"), sem("be_ready")
        var_ready = [sem(f"var_ready{k}") for k in range(LNS)]
        rstd_ready = [sem(f"rstd_ready{k}") for k in range(LNS)]
        xn_ready = [sem(f"xn_ready{k}") for k in range(LNS)]
        xT_psum = [sem(f"xT_psum{k}") for k in range(LNS)]
        xT_hi = [sem(f"xT_hi{k}") for k in range(LNS)]
        xT_lo = [sem(f"xT_lo{k}") for k in range(LNS)]
        q_psum, q_hi, q_lo, m_psum, negmax_ready, nT_psum, nT_ready, e_psum, probs_ready, pv_psum, attn_ready = (
            sem(s) for s in ("q_psum", "q_hi_s", "q_lo_s", "m_psum", "negmax_ready", "nT_psum", "nT_ready", "e_psum",
                             "probs_ready", "pv_psum", "attn_ready"))
        aT_psum, aT_hi, aT_lo, o_psum, xb_ready, x1_ready = (sem(s) for s in (
            "aT_psum", "aT_hi_s", "aT_lo_s", "o_psum", "xb_ready", "x1_ready"))
        logit_psum = [sem(f"logit_psum{k}") for k in range(2)]
        logit_read = [sem(f"logit_read{k}") for k in range(2)]
        shifted = [sem(f"shifted{k}") for k in range(2)]
        exps = [sem(f"exps{k}") for k in range(2)]
        x_psum, x_read = sem("x_psum"), sem("x_read")
        convT_psum, convT_ready, comp_psum, comp_ready, x3_ready = (sem(s) for s in (
            "convT_psum", "convT_ready", "comp_psum", "comp_ready", "x3_ready"))
        rows_in = [sem(f"rows_in{b}") for b in range(B)]
        gate_ready, gT_psum, gT_ready = sem("gate_ready"), sem("gT_psum"), sem("gT_ready")
        h1_psum, h3_psum, gb_psum, silu_ready, gb_ready, gated_ready, hidden_ready = (sem(s) for s in (
            "h1_psum", "h3_psum", "gb_psum", "silu_ready", "gb_ready", "gated_ready", "hidden_ready"))
        y_psum, yT_ready, yt_psum, x4_ready, stored = (sem(s) for s in (
            "y_psum", "yT_ready", "yt_psum", "x4_ready", "stored"))
        dve_step, pool_step = sem("dve_step"), sem("pool_step")

        hi, lo = 0, 1
        LN_OF_T = {"T0": 0, "T1": 1, "T3": 3}

        def xT_of(k, b):
            if k == 3:
                return [x4T_p[s][:, b % 3, :] for s in (hi, lo)]
            return [xT_p[s][:, b % 2, :] for s in (hi, lo)]

        block = es.enter_context(nc.Block())

        @block.sync
        def _(sp):
            x_v = x.rearrange("b (p j) d -> b p (j d)", j=J)
            out_v = out.rearrange("b (p j) d -> b p (j d)", j=J)
            resid_v = resid[:, :, :, :].rearrange("p b j d -> p b (j d)")

            def column(v):
                return v.rearrange("(p a) -> p a", a=1)

            def row(v):
                return v.rearrange("(a n) -> a n", a=1)

            sp.dma_start(resid_v[:, 0, :], x_v[0]).then_inc(ld_x[0], 16)
            sp.dma_start(ctx_sb[:, :], ctx_1024.rearrange("b k d -> (b k) d")).then_inc(ld_ctx, 16)
            sp.dma_start(Wk_sb[:, :], Wk).then_inc(ld_ctx, 16)
            sp.dma_start(bk_col[:, :], column(bk)).then_inc(ld_ctx, 16)
            sp.dma_start(Wv_sb[:, :], Wv).then_inc(ld_ctx, 16)
            sp.wait_ge(zeros_ready, 1)
            sp.dma_start(bv_row[0:1, :], row(bv)).then_inc(ld_ctx, 16)
            sp.dma_start(Wq_sb[:, :], Wq).then_inc(ld_q, 16)
            sp.dma_start(bq_col[:, :], column(bq)).then_inc(ld_q, 16)
            sp.dma_start(Wo_sb[:, :], Wo).then_inc(ld_q, 16)
            sp.dma_start(bo_all[:, :], bo.partition_broadcast(P)).then_inc(ld_q, 16)
            sp.dma_start(resid_v[:, 1, :], x_v[1]).then_inc(ld_x[1], 16)
            sp.dma_start(We_sb[:, :, :], We.rearrange("e d o -> d e o")).then_inc(ld_ffn0, 16)
            sp.dma_start(Wg_sb[:, :], Wg).then_inc(ld_ffn0, 16)
            sp.dma_start(bg_all[:, :], bg.partition_broadcast(P)).then_inc(ld_ffn0, 16)
            sp.dma_start(be_sb[:, :], be.rearrange("(a e) o -> a (e o)", a=1)).then_inc(ld_ffn0, 16)
            sp.dma_start(wr_sb[:, :], w_router).then_inc(ld_ffn0, 16)
            sp.dma_start(conv_sb[:, :, :], conv_w.rearrange("r i o -> i r o")).then_inc(ld_conv, 16)
            sp.dma_start(convb_all[:, :], conv_b.partition_broadcast(COMP)).then_inc(ld_conv, 16)
            for b in range(B):
                sp.dma_start(memory_rows[P - NKEY // J:P, b, :],
                             ctx_1024[b].rearrange("(p j) d -> p (j d)", j=J)).then_inc(rows_in[b], 16)
            sp.dma_start(w1_sb[:, :, :], w1.rearrange("e d h -> d e h")).then_inc(ld_w13, 16)
            sp.dma_start(w3_sb[:, :, :], w3.rearrange("e d h -> d e h")).then_inc(ld_w13, 16)
            for b in range(2, B):
                sp.dma_start(resid_v[:, b, :], x_v[b]).then_inc(ld_x[b], 16)
            sp.dma_start(w2_sb[:, :, :], w2.rearrange("e h d -> (e h) d").rearrange("(c p) d -> p c d", p=P)
                         ).then_inc(ld_w2, 16)
            sp.wait_ge(be_ready, 2)
            sp.dma_start(be_hilo[1:2, :].bitcast(f32), be_lo[:, :].bitcast(f32)).then_inc(be_moved, 16)
            for s, b in steps:
                if s == "memory":
                    sp.wait_ge(xn_ready[2], b + 1)
                    src = xn[:, b % 2, :, :].rearrange("p j d -> p (j d)")
                    up = COMP // J
                    mid = HALF // J
                    old = NKEY // J
                    sp.dma_start(memory_rows[0:mid - up, b, :], src[up:mid, :]).then_inc(rows_in[b], 16)
                    sp.dma_start(memory_rows[mid:P - old, b, :], src[mid + old:P, :]).then_inc(rows_in[b], 16)
                    sp.wait_ge(comp_ready, b + 1)
                    sp.dma_start(memory_rows[mid - up:mid, b, :], comp[:, :]).then_inc(rows_in[b], 16)
                if s == "out":
                    sp.wait_ge(x4_ready, b + 1)
                    sp.dma_start(out_v[b], resid_v[:, b, :]).then_inc(stored, 16)
            sp.wait_ge(stored, 16 * B)

        @block.gpsimd
        def _(pool):
            own = [0]

            def link(ins):
                own[0] += 1
                ins.then_inc(pool_step, 1)
                pool.wait_ge(pool_step, own[0])

            link(pool.memset(ident[:, :], 0.0))
            pool.memset(bv_row[:, :], 0.0).then_inc(zeros_ready, 1)
            link(pool.affine_select(out=ident[:, :], in_=ident[:, :], compare_op=ALU.not_equal, fill=1.0,
                                    base=0, pattern=[[-1, P]], channel_multiplier=1))
            pool.memset(ones[:, :], 1.0)
            pool.memset(minus_half[:, :], -0.5)
            for e in range(E):
                pool.memset(rank_desc[:, :, e:e + 1], float(E - e))
            pool.memset(negmaxT[:, :, :].bitcast(f32), 0.0)
            pool.memset(gateT[:, :, :].bitcast(f32), 0.0)
            pool.memset(be_hilo[:, :].bitcast(f32), 0.0).then_inc(consts_ready, 1)

            def low_part(n, part, whole):
                pool.wait_ge(W_hi, n)
                pool.tensor_tensor(part[lo][:, :], whole, part[hi][:, :].bitcast(f32), ALU.subtract).then_inc(W_lo, 1)

            low_part(1, Wq_p, Wq_sb[:, :])
            low_part(2, Wo_p, Wo_sb[:, :])

            def k_all(b):
                pool.wait_ge(KT_lo, 1)
                pool.wait_ge(masks_ready, 1)
                if b >= 2:
                    pool.wait_ge(e_psum, turn["E3", b - 2])
                for part in (hi, lo):
                    pool.tensor_tensor(K_all[part][:, b % 2, :, :],
                                       KT_p[part][:, b, :].bitcast(f32).unsqueeze(1).broadcast_to([P, H, NKEY]),
                                       head_mask[:, :].unsqueeze(2).broadcast_to([P, H, NKEY]), ALU.mult
                                       ).then_inc(K_all_ready, 1)

            def rstd_of(k, b):
                n = LNS * b + k
                pool.wait_ge(var_ready[k], b + 1)
                link(pool.tensor_scalar(var_eps[:, n, :], mean_var[:, n, :, 1], EPS, 1.0, ALU.add, ALU.mult))
                pool.tensor_tensor(rstd[:, n, :], var_eps[:, n, :], minus_half[:, :], ALU.pow
                                   ).then_inc(rstd_ready[k], 1)

            for s, b in steps:
                if s.startswith("stats"):
                    rstd_of(int(s[5:]), b)
                if s == "norm0":
                    k_all(b)
                if s == "Q":
                    pool.wait_ge(xn_ready[0], b + 1)
                    pool.wait_ge(ld_q, 64)
                    pool.tensor_tensor(resid[:, b, :, :], resid[:, b, :, :],
                                       bo_all[:, :].unsqueeze(1).broadcast_to([P, J, D]), ALU.add
                                       ).then_inc(xb_ready, 1)
                if s == "first_weights":
                    pool.wait_ge(be_ready, 1)
                    low_part(3, Wg_p, Wg_sb[:, :])
                    pool.tensor_tensor(be_lo[:, :], be_sb[:, :], be_hilo[0:1, :].bitcast(f32), ALU.subtract
                                       ).then_inc(be_ready, 1)
                    low_part(4, We_p, We_sb[:, :, :].rearrange("p e o -> p (e o)"))
                if s == "second_weights":
                    low_part(5, w1_p, w1_sb[:, :, :].rearrange("p e h -> p (e h)"))
                    low_part(6, w3_p, w3_sb[:, :, :].rearrange("p e h -> p (e h)"))
                if s == "memory":
                    pool.wait_ge(rows_in[b], 64)
                    pool.tensor_tensor(resid[:, b, :, :].rearrange("p j d -> p (j d)"),
                                       resid[:, b, :, :].rearrange("p j d -> p (j d)"), memory_rows[:, b, :],
                                       ALU.add).then_inc(x3_ready, 1)
                if s[0] == "H":
                    n = NCH * b + int(s[1:])
                    pool.wait_ge(gated_ready, n + 1)
                    pool.wait_ge(gb_ready, n + 1)
                    pool.tensor_tensor(hidden[:, n % 2, :], gated[:, n % 2, :], gate_bc[:, n % 2, :], ALU.mult
                                       ).then_inc(hidden_ready, 1)

        @block.scalar
        def _(act):
            def high_part(part, whole):
                act.activation(part[hi][:, :], whole, ACT.Copy).then_inc(W_hi, 1)

            act.wait_ge(ld_q, 64)
            high_part(Wq_p, Wq_sb[:, :])
            high_part(Wo_p, Wo_sb[:, :])
            act.wait_ge(ctxT_psum, 1)
            act.activation(ctxT[:, :, :, :],
                           bank[0][:, 0:B * NKEY].rearrange("p (b k) -> p b k", b=B).unsqueeze(2)
                           .broadcast_to([P, B, H4, NKEY]), ACT.Copy).then_inc(ctxT_ready, 1)
            act.wait_ge(KT_ready, 1)
            act.activation(KT_p[hi][:, :, :], KT[:, :, :], ACT.Copy).then_inc(KT_hi, 1)

            for s, b in steps:
                par = b % 2
                if s == "first_weights":
                    act.wait_ge(consts_ready, 1)
                    act.activation(ones_r[:, :], ones[:, :], ACT.Copy)
                    act.wait_ge(ld_ffn0, 80)
                    act.activation(be_hilo[0:1, :], be_sb[:, :], ACT.Copy).then_inc(be_ready, 1)
                    high_part(Wg_p, Wg_sb[:, :])
                    high_part(We_p, We_sb[:, :, :].rearrange("p e o -> p (e o)"))
                    act.wait_ge(wr_psum, 1)
                    act.activation(wr_p[hi][:, :], bank[bank_of["first_weights", 0, 0]][:, 0:E], ACT.Copy).then_inc(wr_hi, 1)
                if s == "second_weights":
                    act.wait_ge(ld_w13, 32)
                    high_part(w1_p, w1_sb[:, :, :].rearrange("p e h -> p (e h)"))
                    high_part(w3_p, w3_sb[:, :, :].rearrange("p e h -> p (e h)"))
                if s in LN_OF_T:
                    k = LN_OF_T[s]
                    act.wait_ge(xT_psum[k], b + 1)
                    if k == 3 and b >= 3:
                        act.wait_ge(h3_psum, NCH * (b - 2))
                    act.activation(xT_of(k, b)[hi], bank[bank_of[s, b, 0]][:, :], ACT.Copy).then_inc(xT_hi[k], 1)
                if s == "Q":
                    act.wait_ge(q_psum, b + 1)
                    act.activation(q_p[hi][:, par, :], bank[bank_of[s, b, 0]][:, :], ACT.Identity,
                                   bias=bq_col[:, :]).then_inc(q_hi, 1)
                if s == "negmaxT":
                    act.wait_ge(nT_psum, b + 1)
                    act.activation(negmaxT[0:H, par, :], bank[bank_of[s, b, 0]][0:H, :], ACT.Copy).then_inc(nT_ready, 1)
                if s[0] == "E":
                    c = int(s[1:])
                    act.wait_ge(e_psum, turn[s, b])
                    act.activation(probsT[:, par, c, :], bank[bank_of[s, b, 0]][:, :], ACT.Exp, scale=SCALE
                                   ).then_inc(probs_ready, 1)
                if s == "attnT":
                    act.wait_ge(aT_psum, b + 1)
                    act.activation(aT_p[hi][:, par, :], bank[bank_of[s, b, 0]][:, :], ACT.Copy).then_inc(aT_hi, 1)
                if s[:5] == "route":
                    k = int(s[5:])
                    act.wait_ge(shifted[k], b + 1)
                    act.activation(rt[k][1][:, :, :], rt[k][0][:, :, :], ACT.Exp).then_inc(exps[k], 1)
                if s == "memory":
                    act.wait_ge(convT_psum, b + 1)
                    act.activation(convT[:, :, :], bank[bank_of[s, b, 0]][:, 0:J * COMP], ACT.Copy
                                   ).then_inc(convT_ready, 1)
                if s == "gateT":
                    act.wait_ge(gT_psum, b + 1)
                    if b >= 3:
                        act.wait_ge(gb_psum, NCH * (b - 2))
                    act.activation(gateT[0:2 * E, b % 3, :], bank[bank_of[s, b, 0]][0:2 * E, :], ACT.Copy).then_inc(gT_ready, 1)
                if s[0] == "H":
                    n = NCH * b + int(s[1:])
                    act.wait_ge(h1_psum, n + 1)
                    if n >= 2:
                        act.wait_ge(gated_ready, n - 1)
                    act.activation(silu_h[:, n % 2, :], ps_h1[:, :], ACT.Silu).then_inc(silu_ready, 1)
                    act.wait_ge(gb_psum, n + 1)
                    if n >= 2:
                        act.wait_ge(hidden_ready, n - 1)
                    act.activation(gate_bc[:, n % 2, :], ps_gate[:, :], ACT.Copy).then_inc(gb_ready, 1)
                if s == "out":
                    act.wait_ge(y_psum, b + 1)
                    act.activation(yT, ps_y[:, :], ACT.Copy).then_inc(yT_ready, 1)

        @block.vector
        def _(dve):
            own = [0]

            def link(ins):
                own[0] += 1
                ins.then_inc(dve_step, 1)
                dve.wait_ge(dve_step, own[0])

            dve.wait_ge(consts_ready, 1)
            link(dve.tensor_reduce(head_mask[:, :], ident[:, :].rearrange("p (h k) -> p h k", h=H), AX.X, ALU.add))
            link(dve.tensor_reduce(key_head_mask[:, :], ident[:, :].rearrange("p (h k) -> p h k", h=H4), AX.X, ALU.add))
            dve.tensor_copy(head_rows[:, :, :], ident[:, 0:H].unsqueeze(2).broadcast_to([P, H, NKEY]))
            link(dve.tensor_tensor(expert_mask[:, :], ident[:, 0:E], ident[:, E:2 * E], ALU.add))
            dve.tensor_copy(expert_rows[:, :, :], expert_mask[:, :].unsqueeze(2).broadcast_to([P, E, HID])
                            ).then_inc(masks_ready, 1)
            dve.wait_ge(kv_psum, 2)
            dve.wait_ge(ld_ctx, 80)
            dve.tensor_scalar(KT[:, :, :].rearrange("p b k -> p (b k)"), bank[1][:, 0:B * NKEY], bk_col[:, :], None,
                              ALU.add).then_inc(KT_ready, 1)
            dve.wait_ge(KT_hi, 1)
            dve.tensor_tensor(KT_p[lo][:, :, :], KT[:, :, :], KT_p[hi][:, :, :].bitcast(f32), ALU.subtract
                              ).then_inc(KT_lo, 1)
            v_ps = bank[2][:, :].rearrange("p (b c h k) -> p b c h k", b=B, c=NC4, h=H4)
            for b in range(B):
                last = dve.tensor_tensor(V_aug[:, b, :, :, 0:DK], v_ps[:, b],
                                         key_head_mask[:, :].unsqueeze(1).unsqueeze(3).broadcast_to([P, NC4, H4, DK]),
                                         ALU.mult)
            last.then_inc(V_ready, 1)
            dve.tensor_copy(V_aug[:, :, :, :, DK:VW].rearrange("p b c h a -> p (b c) (h a)"),
                            key_head_mask[:, :].unsqueeze(1).broadcast_to([P, B * NC4, H4])).then_inc(V_ready, 1)

            def route(k, b, ps):
                ex, l, key, one1, l2, d2, one2, sel, picked = rt[k][1], rt[k][2], rt[k][3], rt[k][4], rt[k][5], \
                    rt[k][6], rt[k][7], rt[k][8], rt[k][3]
                d = rt[k][0]
                m1, k1, m2, k2, total, inv = rs[k]

                def bc(v):
                    return v[:, :].unsqueeze(2).broadcast_to([P, J, E])

                def flat(v):
                    return v[:, :, :].rearrange("p j e -> p (j e)")

                dve.wait_ge(logit_psum[k], b + 1)
                psv = ps[:, 0:J * E].rearrange("p (j e) -> p j e", j=J)
                if k == 0:
                    ins = dve.tensor_tensor(l[:, :, :], psv, bg_all[:, :].unsqueeze(1).broadcast_to([P, J, E]), ALU.add)
                else:
                    ins = dve.tensor_copy(l[:, :, :], psv)
                ins.then_inc(logit_read[k], 1)
                dve.wait_ge(logit_read[k], b + 1)
                link(dve.tensor_reduce(m1[:, :], l[:, :, :], AX.X, ALU.max))
                dve.tensor_tensor(d[:, :, :], l[:, :, :], bc(m1), ALU.subtract).then_inc(shifted[k], 1)
                dve.wait_ge(shifted[k], b + 1)
                link(dve.scalar_tensor_tensor(flat(key), flat(d), 0.0, flat(rank_desc), ALU.is_ge, ALU.mult))
                link(dve.tensor_reduce(k1[:, :], key[:, :, :], AX.X, ALU.max))
                link(dve.tensor_tensor(one1[:, :, :], key[:, :, :], bc(k1), ALU.is_equal))
                link(dve.scalar_tensor_tensor(flat(l2), flat(one1), -1e38, flat(d), ALU.mult, ALU.add))
                link(dve.tensor_reduce(m2[:, :], l2[:, :, :], AX.X, ALU.max))
                link(dve.tensor_tensor(d2[:, :, :], l2[:, :, :], bc(m2), ALU.subtract))
                link(dve.scalar_tensor_tensor(flat(key), flat(d2), 0.0, flat(rank_desc), ALU.is_ge, ALU.mult))
                link(dve.tensor_reduce(k2[:, :], key[:, :, :], AX.X, ALU.max))
                link(dve.tensor_tensor(one2[:, :, :], key[:, :, :], bc(k2), ALU.is_equal))
                link(dve.tensor_tensor(sel[:, :, :], one1[:, :, :], one2[:, :, :], ALU.add))
                dve.wait_ge(exps[k], b + 1)
                link(dve.tensor_tensor(picked[:, :, :], ex[:, :, :], sel[:, :, :], ALU.mult))
                link(dve.tensor_reduce(total[:, :], (picked if k == 0 else ex)[:, :, :], AX.X, ALU.add))
                link(dve.reciprocal(inv[:, :], total[:, :]))
                link(dve.tensor_tensor(gate[:, k, b, :, :], picked[:, :, :], bc(inv), ALU.mult))

            for s, b in steps:
                par = b % 2
                if s == "first_weights":
                    dve.wait_ge(wr_hi, 1)
                    dve.tensor_tensor(wr_p[lo][:, :], bank[bank_of["first_weights", 0, 0]][:, 0:E],
                                      wr_p[hi][:, :].bitcast(f32), ALU.subtract).then_inc(wr_lo, 1)
                if s.startswith("stats"):
                    k = int(s[5:])
                    n = LNS * b + k
                    if k == 0:
                        dve.wait_ge(ld_x[b], 16)
                    if k == 1:
                        dve.wait_ge(x1_ready, b + 1)
                    if k == 2:
                        dve.wait_ge(x_read, 2 * turn["X3", b])
                    if k == 3:
                        dve.wait_ge(x3_ready, b + 1)
                    for j in range(J):
                        last = dve.bn_stats(bn[:, n, j, :], resid[:, b, j, :])
                    link(last)
                    for j in range(J):
                        last = dve.bn_aggr(mean_var[:, n, j, :], bn[:, n, j, :])
                    last.then_inc(var_ready[k], 1)
                if s.startswith("norm"):
                    k = int(s[4:])
                    n = LNS * b + k
                    dve.wait_ge(rstd_ready[k], b + 1)
                    for j in range(J):
                        last = dve.tensor_scalar(xn[:, par, j, :], resid[:, b, j, :], mean_var[:, n, j, 0:1],
                                                 rstd[:, n, j:j + 1], ALU.subtract, ALU.mult)
                    last.then_inc(xn_ready[k], 1)
                if s in LN_OF_T:
                    k = LN_OF_T[s]
                    dve.wait_ge(xT_hi[k], b + 1)
                    dve.tensor_tensor(xT_of(k, b)[lo], bank[bank_of[s, b, 0]][:, :], xT_of(k, b)[hi].bitcast(f32),
                                      ALU.subtract).then_inc(xT_lo[k], 1)
                if s == "Q":
                    dve.wait_ge(q_hi, b + 1)
                    dve.scalar_tensor_tensor(q_p[lo][:, par, :], bank[bank_of[s, b, 0]][:, :], bq_col[:, :],
                                             q_p[hi][:, par, :].bitcast(f32), ALU.add, ALU.subtract).then_inc(q_lo, 1)
                if s[0] == "M":
                    j = int(s[1:])
                    dve.wait_ge(m_psum, turn[s, b])
                    dve.tensor_reduce(negmax[:, par, j, :],
                                      bank[bank_of[s, b, 0]][:, :].rearrange("p (h k) -> p h k", h=H),
                                      AX.X, ALU.max, negate=True).then_inc(negmax_ready, 1)
                if s == "V":
                    for g in range(2):
                        ps = bank[bank_of[s, b, g]][:, 0:2 * H * VW].rearrange("p (h v) -> p h v", v=VW)
                        dve.wait_ge(pv_psum, 2 * b + g + 1)
                        link(dve.reciprocal(rden[:, g, :], ps[:, :, DK]))
                        dve.tensor_tensor(attn[:, par, 2 * g:2 * g + 2, :, :].rearrange("p j h k -> p (j h) k"),
                                          ps[:, :, 0:DK], rden[:, g, :].unsqueeze(2).broadcast_to([P, 2 * H, DK]),
                                          ALU.mult).then_inc(attn_ready, 1)
                if s == "attnT":
                    dve.wait_ge(aT_hi, b + 1)
                    dve.tensor_tensor(aT_p[lo][:, par, :], bank[bank_of[s, b, 0]][:, :],
                                      aT_p[hi][:, par, :].bitcast(f32), ALU.subtract).then_inc(aT_lo, 1)
                if s == "O":
                    dve.wait_ge(o_psum, b + 1)
                    dve.wait_ge(xb_ready, b + 1)
                    dve.tensor_tensor(resid[:, b, :, :].rearrange("p j d -> p (j d)"), bank[bank_of[s, b, 0]][:, :],
                                      resid[:, b, :, :].rearrange("p j d -> p (j d)"), ALU.add).then_inc(x1_ready, 1)
                if s[:5] == "route":
                    k = int(s[5:])
                    if k == 0 and b == 0:
                        dve.wait_ge(ld_ffn0, 80)
                    route(k, b, bank[bank_of[s, b, 0]])
                    if k == 1:
                        link(dve.tensor_copy(gate_hilo[:, b, :, 0:E], gate[:, 1, b, :, :]))
                        dve.tensor_tensor(gate_hilo[:, b, :, E:2 * E], gate[:, 1, b, :, :],
                                          gate_hilo[:, b, :, 0:E].bitcast(f32), ALU.subtract).then_inc(gate_ready, 1)
                if s[0] == "X":
                    j = int(s[1:])
                    for g in range(2):
                        n = 2 * (turn[s, b] - 1) + g
                        dve.wait_ge(x_psum, n + 1)
                        for i in range(E // 2):
                            e = E // 2 * g + i
                            ins = dve.scalar_tensor_tensor(resid[:, b, j, :], bank[bank_of[s, b, g]][:, D * i:D * i + D],
                                                           gate[:, 0, b, j, e:e + 1], resid[:, b, j, :],
                                                           ALU.mult, ALU.add)
                            if i < E // 2 - 1:
                                link(ins)
                        ins.then_inc(x_read, 1)
                        dve.wait_ge(x_read, n + 1)
                if s == "memory":
                    dve.wait_ge(comp_psum, b + 1)
                    if b == 0:
                        dve.wait_ge(ld_conv, 32)
                    if b >= 1:
                        dve.wait_ge(rows_in[b - 1], 64)
                    dve.tensor_tensor(comp[:, :], bank[bank_of[s, b, 1]][0:COMP, 0:D], convb_all[:, :], ALU.add
                                      ).then_inc(comp_ready, 1)
                if s[0] == "H":
                    n = NCH * b + int(s[1:])
                    dve.wait_ge(silu_ready, n + 1)
                    dve.wait_ge(h3_psum, n + 1)
                    if n >= 2:
                        dve.wait_ge(hidden_ready, n - 1)
                    dve.tensor_tensor(gated[:, n % 2, :], ps_h3[n % 2][:, :], silu_h[:, n % 2, :], ALU.mult
                                      ).then_inc(gated_ready, 1)
                if s == "out":
                    dve.wait_ge(yt_psum, b + 1)
                    dve.tensor_tensor(resid[:, b, :, :].rearrange("p j d -> p (j d)"), bank[bank_of[s, b, 0]][:, :],
                                      resid[:, b, :, :].rearrange("p j d -> p (j d)"), ALU.add).then_inc(x4_ready, 1)

        @block.tensor
        def _(pe):
            last_reader = {}

            def take(s, b, i, reader, count):
                k = bank_of[s, b, i]
                if k in last_reader:
                    pe.wait_ge(*last_reader[k])
                last_reader[k] = (reader, count)
                return bank[k]

            def three_passes(o, lhs, rhs, start=True, stop=True):
                pe.matmul(o, lhs[hi], rhs[hi], start=start, stop=False)
                pe.matmul(o, lhs[lo], rhs[hi], start=False, stop=False)
                return pe.matmul(o, lhs[hi], rhs[lo], start=False, stop=stop)

            pe.wait_ge(consts_ready, 1)
            pe.wait_ge(ld_ctx, 80)
            ps = take("setup", 0, 0, ctxT_ready, 1)
            pe.transpose(ps[:, 0:P], ctx_sb[:, :], ident[:, :]).then_inc(ctxT_psum, 1)
            pe.wait_ge(ctxT_ready, 1)
            ps = take("setup", 0, 1, KT_ready, 1)
            pe.matmul(ps[:, 0:P], Wk_sb[:, :], ctxT[:, :, 0, :], start=True, stop=True).then_inc(kv_psum, 1)
            ps = take("setup", 0, 2, V_ready, 2)
            for b in range(B):
                pe.matmul(ps[:, D * b:D * b + D], ctxT[:, b, :, :].rearrange("p h k -> p (h k)"), Wv_sb[:, :],
                          start=True, stop=False)
                last = pe.matmul(ps[:, D * b:D * b + D], ones[:, :], bv_row[:, :], start=False, stop=True)
            last.then_inc(kv_psum, 1)

            def y_product(n):
                c = n % NCH
                b = n // NCH
                pe.wait_ge(hidden_ready, n + 1)
                if c == 0 and b >= 1:
                    pe.wait_ge(yT_ready, b)
                ins = pe.matmul(ps_y[:, :], w2_sb[:, c, :], hidden[:, n % 2, :], start=(c == 0), stop=(c == NCH - 1))
                if c == NCH - 1:
                    ins.then_inc(y_psum, 1)

            for s, b in steps:
                par = b % 2
                if s in LN_OF_T:
                    k = LN_OF_T[s]
                    ps = take(s, b, 0, xT_lo[k], b + 1)
                    pe.wait_ge(xn_ready[k], b + 1)
                    for j in range(J):
                        last = pe.transpose(ps[:, P * j:P * j + P], xn[:, par, j, :], ident[:, :])
                    last.then_inc(xT_psum[k], 1)
                if s == "first_weights":
                    ps = take(s, b, 0, wr_lo, 1)
                    pe.wait_ge(ld_ffn0, 80)
                    pe.transpose(ps[:, 0:E], wr_sb[:, :], ident[0:E, 0:E]).then_inc(wr_psum, 1)
                if s == "Q":
                    ps = take(s, b, 0, q_lo, b + 1)
                    pe.wait_ge(W_lo, 2)
                    pe.wait_ge(xT_lo[0], b + 1)
                    three_passes(ps[:, :], [w[:, :] for w in Wq_p], xT_of(0, b)).then_inc(q_psum, 1)
                if s[0] == "M":
                    j = int(s[1:])
                    ps = take(s, b, 0, negmax_ready, turn[s, b])
                    pe.wait_ge(q_hi, b + 1)
                    pe.wait_ge(K_all_ready, 2 * (b + 1))
                    pe.matmul(ps[:, :], q_p[hi][:, par, P * j:P * j + P],
                              K_all[hi][:, par, :, :].rearrange("p h k -> p (h k)"), start=True, stop=True
                              ).then_inc(m_psum, 1)
                if s == "negmaxT":
                    ps = take(s, b, 0, nT_ready, b + 1)
                    pe.wait_ge(negmax_ready, turn["M3", b])
                    for j in range(J):
                        last = pe.transpose(ps[0:H, P * j:P * j + P], negmax[:, par, j, :], ident[:, :])
                    last.then_inc(nT_psum, 1)
                if s[0] == "E":
                    c = int(s[1:])
                    ps = take(s, b, 0, probs_ready, turn[s, b])
                    pe.wait_ge(nT_ready, b + 1)
                    pe.wait_ge(q_lo, b + 1)
                    three_passes(ps[:, :], [w[:, par, H4 * c:H4 * c + H4, :].rearrange("p h k -> p (h k)") for w in K_all],
                                 [q[:, par, :] for q in q_p], stop=False)
                    pe.matmul(ps[:, :], head_rows[:, H4 * c:H4 * c + H4, :].rearrange("g h k -> g (h k)"),
                              negmaxT[:, par, :], start=False, stop=True).then_inc(e_psum, 1)
                if s == "V":
                    for g in range(2):
                        ps = take(s, b, g, attn_ready, 2 * b + g + 1)
                        pe.wait_ge(probs_ready, turn["E3", b])
                        pe.wait_ge(V_ready, 2)
                        for i in range(2):
                            j = 2 * g + i
                            for c in range(NC4):
                                at = i * H * VW + c * H4 * VW
                                last = pe.matmul(ps[:, at:at + H4 * VW], probsT[:, par, c, P * j:P * j + P],
                                                 V_aug[:, b, c, :, :].rearrange("p h v -> p (h v)"),
                                                 start=True, stop=True)
                        last.then_inc(pv_psum, 1)
                if s == "attnT":
                    ps = take(s, b, 0, aT_lo, b + 1)
                    pe.wait_ge(attn_ready, 2 * (b + 1))
                    for j in range(J):
                        last = pe.transpose(ps[:, P * j:P * j + P],
                                            attn[:, par, j, :, :].rearrange("p h k -> p (h k)"), ident[:, :])
                    last.then_inc(aT_psum, 1)
                if s == "O":
                    ps = take(s, b, 0, x1_ready, b + 1)
                    pe.wait_ge(aT_lo, b + 1)
                    for j in range(J):
                        last = three_passes(ps[:, D * j:D * j + D], [a[:, par, P * j:P * j + P] for a in aT_p],
                                            [w[:, :] for w in Wo_p])
                    last.then_inc(o_psum, 1)
                if s[:5] == "route":
                    k = int(s[5:])
                    ln = 1 if k == 0 else 3
                    ps = take(s, b, 0, logit_read[k], b + 1)
                    pe.wait_ge(xT_lo[ln], b + 1)
                    if k == 0:
                        pe.wait_ge(W_lo, 3)
                    else:
                        pe.wait_ge(wr_lo, 1)
                    for j in range(J):
                        last = three_passes(ps[:, E * j:E * j + E], [a[:, P * j:P * j + P] for a in xT_of(ln, b)],
                                            [w[:, :] for w in (Wg_p if k == 0 else wr_p)])
                    last.then_inc(logit_psum[k], 1)
                if s[0] == "X":
                    j = int(s[1:])
                    for g in range(2):
                        n = 2 * (turn[s, b] - 1) + g
                        cols = slice(D * E // 2 * g, D * E // 2 * (g + 1))
                        ps = take(s, b, g, x_read, n + 1)
                        pe.wait_ge(W_lo, 4)
                        pe.wait_ge(be_moved, 16)
                        three_passes(ps[:, :], [a[:, P * j:P * j + P] for a in xT_of(1, b)],
                                     [w[:, cols] for w in We_p], stop=False)
                        pe.matmul(ps[:, :], ones_r[:, :], be_hilo[:, cols], start=False, stop=True).then_inc(x_psum, 1)
                if s == "memory":
                    ps = take(s, b, 0, convT_ready, b + 1)
                    pe.wait_ge(xn_ready[2], b + 1)
                    at = HALF // J
                    for j in range(J):
                        last = pe.transpose(ps[:, COMP * j:COMP * j + COMP], xn[at:at + COMP, par, j, :],
                                            ident[at:at + COMP, at:at + COMP])
                    last.then_inc(convT_psum, 1)
                    ps = take(s, b, 1, comp_ready, b + 1)
                    pe.wait_ge(convT_ready, b + 1)
                    pe.wait_ge(ld_conv, 32)
                    for j in range(J):
                        last = pe.matmul(ps[0:COMP, 0:D], convT[:, j, :], conv_sb[:, j, :],
                                         start=(j == 0), stop=(j == J - 1))
                    last.then_inc(comp_psum, 1)
                if s == "gateT":
                    ps = take(s, b, 0, gT_ready, b + 1)
                    pe.wait_ge(gate_ready, b + 1)
                    for j in range(J):
                        last = pe.transpose(ps[0:2 * E, P * j:P * j + P], gate_hilo[:, b, j, :].bitcast(f32), ident[:, :])
                    last.then_inc(gT_psum, 1)
                if s[0] == "H":
                    c = int(s[1:])
                    n = NCH * b + c
                    cols = slice(P * c, P * c + P)
                    if n == 0:
                        pe.wait_ge(W_lo, 6)
                        pe.wait_ge(ld_w2, 16)
                        pe.wait_ge(masks_ready, 1)
                    pe.wait_ge(xT_lo[3], b + 1)
                    if n >= 1:
                        pe.wait_ge(silu_ready, n)
                    three_passes(ps_h1[:, :], [w[:, cols] for w in w1_p], xT_of(3, b)).then_inc(h1_psum, 1)
                    if n >= 2:
                        pe.wait_ge(gated_ready, n - 1)
                    three_passes(ps_h3[n % 2][:, :], [w[:, cols] for w in w3_p], xT_of(3, b)).then_inc(h3_psum, 1)
                    pe.wait_ge(gT_ready, b + 1)
                    if n >= 1:
                        pe.wait_ge(gb_ready, n)
                    pe.matmul(ps_gate[:, :], expert_rows[:, :, :].rearrange("g e h -> g (e h)")[:, cols],
                              gateT[:, b % 3, :], start=True, stop=True).then_inc(gb_psum, 1)
                    if c >= 1:
                        y_product(n - 1)
                if s == "out":
                    y_product(NCH * (b + 1) - 1)
                    pe.wait_ge(yT_ready, b + 1)
                    ps = take(s, b, 0, x4_ready, b + 1)
                    for j in range(J):
                        last = pe.transpose(ps[:, P * j:P * j + P], yT[:, P * j:P * j + P], ident[:, :])
                    last.then_inc(yt_psum, 1)


_INS = ['x', 'ctx_1024', 'L0_xattn_Wq', 'L0_xattn_bq', 'L0_xattn_Wk', 'L0_xattn_bk', 'L0_xattn_Wv', 'L0_xattn_bv',
        'L0_xattn_Wo', 'L0_xattn_bo', 'L0_ffn_We', 'L0_ffn_be', 'L0_ffn_Wg', 'L0_ffn_bg', 'L1_xattn_conv_w',
        'L1_xattn_conv_b', 'L1_ffn_w_router', 'L1_ffn_w1', 'L1_ffn_w2', 'L1_ffn_w3']
_OUTS = [((4, 512, 128), 'float32')]


def kernel(**inputs):
    import numpy as _np
    import concourse.bacc as _bacc
    from concourse import mybir as _mybir
    from concourse.bass_utils import run_bass_kernel_spmd as _run

    nc = _bacc.Bacc("TRN2", target_bir_lowering=False, num_devices=1)
    arrays, args = {}, []
    for name in _INS:
        a = _np.ascontiguousarray(inputs[name])
        arrays[f"in_{name}_dram"] = a
        args.append(nc.dram_tensor(f"in_{name}_dram", a.shape, _mybir.dt.from_np(a.dtype), kind="ExternalInput").ap())
    for i, (shape, dtype) in enumerate(_OUTS):
        dt = _mybir.dt.from_np(_np.dtype(dtype))
        args.append(nc.dram_tensor(f"out_{i}_dram", shape, dt, kind="ExternalOutput").ap())
    block_program(nc, *args)
    r = _run(nc, [arrays], core_ids=[0])
    got = tuple(r.results[0][f"out_{i}_dram"] for i in range(len(_OUTS)))
    return got[0]
```

```python
import concourse.bass as bass
from concourse import mybir
from contextlib import ExitStack



GROUP = 1


def order_of_steps(batches, chunks, group=GROUP):
    SLOTS = 4
    ln_gap = 3.5

    def prepared(b, start, stretch, gap):
        t, out = start, []

        def at(kind, i, took):
            nonlocal t
            out.append((t, (kind, b, i)))
            t += took * stretch

        def layer_norm(k):
            at("stats", k, 1.5)
            at("norm", k, ln_gap - 1.5)
        layer_norm(0)
        at("keys", 0, 0)
        at("T", 0, 1.2)
        at("Q", 0, 1.8)
        for j in range(SLOTS):
            at("max", j, 0.6)
        at("maxT", 0, 1.2)
        t += gap
        for c in range(SLOTS):
            at("exp", c, 0.05)
        t += 3
        at("V", 0, 1.7)
        at("V", 1, 2)
        at("attnT", 0, 1.2)
        at("O", 0, 1.5)
        layer_norm(1)
        at("T", 1, 1.7)
        if b % group == group - 1:
            at("route", 0, 4.5)
        for i in range(SLOTS):
            at("X", i, 2.1)
        layer_norm(2)
        at("conv", 0, 2)
        at("rows", 0, 3)
        layer_norm(3)
        at("T", 3, 1.7)
        if b % group == group - 1:
            at("route", 1, 4.5)
        at("gateT", 0, 1.5)
        return out, t

    def hidden(b, start, pitch):
        t, out = start, []
        for c in range(chunks):
            out += [(t, ("h1", b, c)), (t + 0.3 * pitch, ("h3", b, c)), (t + 0.6 * pitch, ("gate", b, c))]
            t += pitch
            out.append((t - 0.3 * pitch + 1.0 * pitch, ("y", b, c)))
        out.append((t + pitch, ("out", b, 0)))
        return out, t

    plan, free, ended = [], 0, []
    for b in range(batches):
        start, stretch, gap = PREPARE[b]
        if b >= 2:
            start = max(start, ended[b - 2] + 0.1)
        part, ready = prepared(b, start, stretch, gap)
        ended.append(ready)
        plan += part
        part, free = hidden(b, max(free, ready), PITCH[b])
        plan += part
    plan.append((FIRST_WEIGHTS, ("first_weights", 0, 0)))
    plan.append((SECOND_WEIGHTS, ("second_weights", 0, 0)))
    return [step for _, step in sorted(plan, key=lambda p: p[0])]


PREPARE = [(0, 0.95, 0), (7, 1.1, 0), (45, 1.3, 3), (75, 1.3, 0)]
PITCH = [3.4, 3.4, 2.41, 2.4]
FIRST_WEIGHTS = 12
SECOND_WEIGHTS = 40


def block_program(nc, x, ctx_1024, Wq, bq, Wk, bk, Wv, bv, Wo, bo, We, be, Wg, bg, conv_w, conv_b,
                  w_router, w1, w2, w3, out):
    f32 = mybir.dt.float32
    f32r = mybir.dt.float32r
    ALU = mybir.AluOpType
    ACT = mybir.ActivationFunctionType
    AX = mybir.AxisListType

    B, S, D = x.shape
    NKEY = ctx_1024.shape[1]
    H = 16
    DK = D // H
    E = We.shape[0]
    HID = w1.shape[2]
    P = 128
    J = S // P
    NC4 = H * NKEY // P
    H4 = H // NC4
    EH = E * HID
    NCH = EH // P
    KC = P // NC4
    VW = DK + 1
    CONV = conv_w.shape[0]
    HALF = S // 2
    COMP = NKEY // CONV
    EPS = 1e-5
    SCALE = float(DK) ** -0.5
    LNS = 4
    assert CONV == J and D == P and NC4 * KC == P

    steps = order_of_steps(B, NCH)

    NBANKS, NSHARED = 8, 3
    uses = {"T": 1, "Q": 1, "max": 1, "maxT": 1, "exp": 1, "V": 1, "attnT": 1, "O": 1, "route": 1, "X": 2,
            "conv": 2, "gateT": 1, "out": 1, "first_weights": 1}
    SETUP_USES = 3
    bank_of = {("setup", 0, 0, i): i for i in range(SETUP_USES)}
    n = SETUP_USES
    gated_from = next(i for i, step in enumerate(steps) if step[0] == "h1")
    for at, step in enumerate(steps):
        for i in range(uses.get(step[0], 0)):
            bank_of[(*step, i)] = n % (NBANKS if at < gated_from else NSHARED)
            n += 1

    turn, come = {}, {}
    for step in steps:
        come[step[0]] = turn[step] = come.get(step[0], 0) + 1

    es = ExitStack()
    with es:
        def sb(name, shape, dt=f32):
            return es.enter_context(nc.sbuf_tensor(name, shape, dt))

        def sem(name):
            return es.enter_context(nc.semaphore(name))

        ident = sb("ident", [P, P])
        ones = sb("ones", [P, P])
        minus_half = sb("minus_half", [P, J])
        rank_desc = sb("rank_desc", [P, GROUP * J, E])
        head_mask = sb("head_mask", [P, H])
        key_head_mask = sb("key_head_mask", [P, H4])
        head_rows = sb("head_rows", [P, H, NKEY], f32r)
        expert_mask = sb("expert_mask", [P, E])
        expert_rows = sb("expert_rows", [P, E, HID], f32r)
        ones_r = sb("ones_r", [P, P], f32r)

        ctx_sb = sb("ctx_sb", [P, D])
        ctxT = sb("ctxT", [P, B, H4, NKEY])
        Wk_sb = sb("Wk_sb", [P, D])
        Wv_sb = sb("Wv_sb", [P, D])
        Wq_sb = sb("Wq_sb", [P, D])
        Wo_sb = sb("Wo_sb", [P, D])
        bk_col = sb("bk_col", [P, 1])
        bq_col = sb("bq_col", [P, 1])
        bv_row = sb("bv_row", [P, D])
        bo_all = sb("bo_all", [P, D])
        bg_all = sb("bg_all", [P, E])
        convb_all = sb("convb_all", [COMP, D])
        We_sb = sb("We_sb", [P, E, D])
        Wg_sb = sb("Wg_sb", [P, E])
        be_sb = sb("be_sb", [1, E * D])
        conv_sb = sb("conv_sb", [P, CONV, D])
        wr_sb = sb("wr_sb", [E, D])
        w1_sb = sb("w1_sb", [P, E, HID])
        w3_sb = sb("w3_sb", [P, E, HID])
        w2_sb = sb("w2_sb", [P, NCH, D])
        router_hilo = [sb(f"router{k}_hilo", [P, 2, E], f32r) for k in range(2)]
        router_hi0 = [sb(f"router{k}_hi0", [P, 2, E], f32r) for k in range(2)]
        We_p = [sb(f"We_{s}", [P, E * D], f32r) for s in ("hi", "lo")]
        w1_p = [sb(f"w1_{s}", [P, EH], f32r) for s in ("hi", "lo")]
        w3_p = [sb(f"w3_{s}", [P, EH], f32r) for s in ("hi", "lo")]
        be_hilo = sb("be_hilo", [P, E * D], f32r)
        be_lo = sb("be_lo", [1, E * D], f32r)
        KT = sb("KT", [P, B, NKEY])
        KT_p = [sb(f"KT_{s}", [P, B, NKEY], f32r) for s in ("hi", "lo")]
        K_all = [sb(f"K_all_{s}", [P, 2, H, NKEY], f32r) for s in ("hi", "lo")]
        V_aug = sb("V_aug", [P, B, NC4, H4, VW])

        resid = sb("resid", [P, B, J, D])
        memory_rows = sb("memory_rows", [P, B, J * D])
        bn = sb("bn", [P, LNS * B, J, 6])
        mean_var = sb("mean_var", [P, LNS * B, J, 2])
        var_eps = sb("var_eps", [P, LNS * B, J])
        rstd = sb("rstd", [P, LNS * B, J])
        neg_mean = sb("neg_mean", [P, LNS * B, J])
        neg_mean_rstd = sb("neg_mean_rstd", [P, LNS * B, J])
        xn = sb("xn", [P, 2, J, D])
        x1T = sb("x1T", [P, 2, S])
        xT_p = [sb(f"xT_{s}", [P, 2, S], f32r) for s in ("hi", "lo")]
        x4T_p = [sb(f"x4T_{s}", [P, 3, S], f32r) for s in ("hi", "lo")]
        q_p = [sb(f"q_{s}", [P, 2, S], f32r) for s in ("hi", "lo")]
        negmax = sb("negmax", [P, 2, J, H])
        negmaxT = sb("negmaxT", [P, 2, S], f32r)
        probsT = sb("probsT", [P, 2, NC4, S])
        rden = sb("rden", [P, 4, 2 * H])
        attn = sb("attn", [P, 2, J, H, DK])
        aT = sb("aT", [P, 2, S])
        rt = [[sb(f"rt{k}_{i}", [P, GROUP * J, E]) for i in range(9)] for k in range(2)]
        rs = [[sb(f"rs{k}_{i}", [P, GROUP * J]) for i in range(6)] for k in range(2)]
        gate = sb("gate", [P, 2, B, J, E])
        gate_hilo = sb("gate_hilo", [P, B, J, 2 * E], f32r)
        gateT = sb("gateT", [P, 3, S], f32r)
        convT = sb("convT", [P, 2, J, COMP])
        comp = sb("comp", [COMP, 2, D])
        silu_h = sb("silu_h", [P, 2, S])
        gate_bc = sb("gate_bc", [P, 2, S])
        gated = sb("gated", [P, 2, S])
        hidden = sb("hidden", [P, 2, S])
        yT = We_sb[:, 0:J, :].rearrange("p e o -> p (e o)")

        bank = [es.enter_context(nc.psum_tensor(f"bank{i}", [P, S], f32)) for i in range(NBANKS)]
        H1_BANK, H3_BANKS, GATE_BANK, Y_BANK = 3, (4, 5), 6, 7
        ps_h1, ps_gate, ps_y = bank[H1_BANK], bank[GATE_BANK], bank[Y_BANK]
        ps_h3 = [bank[k] for k in H3_BANKS]

        ld_ctx, ld_q, ld_ffn0, ld_conv, ld_w13, ld_w2 = (sem(s) for s in (
            "ld_ctx", "ld_q", "ld_ffn0", "ld_conv", "ld_w13", "ld_w2"))
        ld_x = [sem(f"ld_x{b}") for b in range(B)]
        be_moved = sem("be_moved")
        consts_ready, zeros_ready, masks_ready = sem("consts_ready"), sem("zeros_ready"), sem("masks_ready")
        ctxT_psum, ctxT_ready, kv_psum, KT_ready, KT_hi, KT_lo, K_all_ready, V_ready = (sem(s) for s in (
            "ctxT_psum", "ctxT_ready", "kv_psum", "KT_ready", "KT_hi_s", "KT_lo_s", "K_all_ready", "V_ready"))
        wr_psum, wr_hi, wr_lo = sem("wr_psum"), sem("wr_hi"), sem("wr_lo")
        W_hi, W_lo, be_ready = sem("W_hi"), sem("W_lo"), sem("be_ready")
        var_ready, rstd_ready, shift_ready, xn_dve, xn_act = (sem(s) for s in (
            "var_ready", "rstd_ready", "shift_ready", "xn_dve", "xn_act"))
        xT_psum, xT_hi, xT_lo = sem("xT_psum"), sem("xT_hi_s"), sem("xT_lo_s")
        q_psum, q_hi, q_lo, m_psum, negmax_ready, nT_psum, nT_ready, e_psum, probs_ready, pv_psum, attn_ready = (
            sem(s) for s in ("q_psum", "q_hi_s", "q_lo_s", "m_psum", "negmax_ready", "nT_psum", "nT_ready", "e_psum",
                             "probs_ready", "pv_psum", "attn_ready"))
        aT_psum, aT_ready, o_psum, xb_ready, x1_ready = (sem(s) for s in (
            "aT_psum", "aT_ready", "o_psum", "xb_ready", "x1_ready"))
        logit_psum = sem("logit_psum")
        logit_read = sem("logit_read")
        shifted = sem("shifted")
        exps = sem("exps")
        x_psum, x_read = sem("x_psum"), sem("x_read")
        convT_psum, convT_ready, comp_psum, comp_ready, x3_ready = (sem(s) for s in (
            "convT_psum", "convT_ready", "comp_psum", "comp_ready", "x3_ready"))
        rows_in = [sem(f"rows_in{b}") for b in range(B)]
        gate_ready, gT_psum, gT_ready = sem("gate_ready"), sem("gT_psum"), sem("gT_ready")
        h1_psum, h3_psum, gb_psum, silu_ready, gb_ready, gated_ready, hidden_ready = (sem(s) for s in (
            "h1_psum", "h3_psum", "gb_psum", "silu_ready", "gb_ready", "gated_ready", "hidden_ready"))
        y_psum, yT_ready, yt_psum, x4_ready, stored = (sem(s) for s in (
            "y_psum", "yT_ready", "yt_psum", "x4_ready", "stored"))
        dve_step, pool_step = sem("dve_step"), sem("pool_step")

        hi, lo = 0, 1
        NORM_V = J // 2

        def split_xT(k, b):
            if k == 3:
                return [x4T_p[s][:, b % 3, :] for s in (hi, lo)]
            return [xT_p[s][:, b % 2, :] for s in (hi, lo)]

        def xn_read_by(b, k):
            if k == 0:
                return ("T", b - 2, 3) if b >= 2 else None
            return ("T", b, k - 1) if k < 3 else None

        def xT_splits(b, k):
            return sum(t[0] == "T" and t[2] > 0 and turn[t] <= turn["T", b, k] for t in turn)

        def ps_of(step, i=0):
            return bank[bank_of[(*step, i)]]

        def flat(v):
            names = " ".join("abcd"[:len(v.shape) - 1])
            return v.rearrange(f"p {names} -> p ({names})")

        block = es.enter_context(nc.Block())

        @block.sync
        def _(sp):
            x_v = x.rearrange("b (p j) d -> b p (j d)", j=J)
            out_v = out.rearrange("b (p j) d -> b p (j d)", j=J)
            resid_v = resid[:, :, :, :].rearrange("p b j d -> p b (j d)")

            def column(v):
                return v.rearrange("(p a) -> p a", a=1)

            def row(v):
                return v.rearrange("(a n) -> a n", a=1)

            sp.dma_start(resid_v[:, 0, :], x_v[0]).then_inc(ld_x[0], 16)
            sp.dma_start(ctx_sb[:, :], ctx_1024.rearrange("b k d -> (b k) d")).then_inc(ld_ctx, 16)
            sp.dma_start(Wk_sb[:, :], Wk).then_inc(ld_ctx, 16)
            sp.dma_start(bk_col[:, :], column(bk)).then_inc(ld_ctx, 16)
            sp.dma_start(Wv_sb[:, :], Wv).then_inc(ld_ctx, 16)
            sp.wait_ge(zeros_ready, 1)
            sp.dma_start(bv_row[0:1, :], row(bv)).then_inc(ld_ctx, 16)
            sp.dma_start(Wq_sb[:, :], Wq).then_inc(ld_q, 16)
            sp.dma_start(bq_col[:, :], column(bq)).then_inc(ld_q, 16)
            sp.dma_start(Wo_sb[:, :], Wo).then_inc(ld_q, 16)
            sp.dma_start(bo_all[:, :], bo.partition_broadcast(P)).then_inc(ld_q, 16)
            sp.dma_start(resid_v[:, 1, :], x_v[1]).then_inc(ld_x[1], 16)
            sp.dma_start(We_sb[:, :, :], We.rearrange("e d o -> d e o")).then_inc(ld_ffn0, 16)
            sp.dma_start(Wg_sb[:, :], Wg).then_inc(ld_ffn0, 16)
            sp.dma_start(bg_all[:, :], bg.partition_broadcast(P)).then_inc(ld_ffn0, 16)
            sp.dma_start(be_sb[:, :], be.rearrange("(a e) o -> a (e o)", a=1)).then_inc(ld_ffn0, 16)
            sp.dma_start(wr_sb[:, :], w_router).then_inc(ld_ffn0, 16)
            sp.dma_start(conv_sb[:, :, :], conv_w.rearrange("r i o -> i r o")).then_inc(ld_conv, 16)
            sp.dma_start(convb_all[:, :], conv_b.partition_broadcast(COMP)).then_inc(ld_conv, 16)
            for b in range(B):
                sp.dma_start(memory_rows[P - NKEY // J:P, b, :],
                             ctx_1024[b].rearrange("(p j) d -> p (j d)", j=J)).then_inc(rows_in[b], 16)
            sp.dma_start(w1_sb[:, :, :], w1.rearrange("e d h -> d e h")).then_inc(ld_w13, 16)
            sp.dma_start(w3_sb[:, :, :], w3.rearrange("e d h -> d e h")).then_inc(ld_w13, 16)
            for b in range(2, B):
                sp.dma_start(resid_v[:, b, :], x_v[b]).then_inc(ld_x[b], 16)
            sp.dma_start(w2_sb[:, :, :], w2.rearrange("e h d -> (e h) d").rearrange("(c p) d -> p c d", p=P)
                         ).then_inc(ld_w2, 16)
            sp.wait_ge(be_ready, 2)
            sp.dma_start(be_hilo[1:2, :].bitcast(f32), be_lo[:, :].bitcast(f32)).then_inc(be_moved, 16)
            for step in steps:
                kind, b, i = step
                if kind == "rows":
                    sp.wait_ge(xn_dve, turn["norm", b, 2])
                    sp.wait_ge(xn_act, turn["norm", b, 2])
                    src = flat(xn[:, b % 2, :, :])
                    up, mid, old = COMP // J, HALF // J, NKEY // J
                    sp.dma_start(memory_rows[0:mid - up, b, :], src[up:mid, :]).then_inc(rows_in[b], 16)
                    sp.dma_start(memory_rows[mid:P - old, b, :], src[mid + old:P, :]).then_inc(rows_in[b], 16)
                    sp.wait_ge(comp_ready, turn["conv", b, 0])
                    sp.dma_start(memory_rows[mid - up:mid, b, :], comp[:, b % 2, :]).then_inc(rows_in[b], 16)
                if kind == "out":
                    sp.wait_ge(x4_ready, b + 1)
                    sp.dma_start(out_v[b], resid_v[:, b, :]).then_inc(stored, 16)
            sp.wait_ge(stored, 16 * B)

        @block.gpsimd
        def _(pool):
            own = [0]

            def link(ins):
                own[0] += 1
                ins.then_inc(pool_step, 1)
                pool.wait_ge(pool_step, own[0])

            link(pool.memset(ident[:, :], 0.0))
            pool.memset(bv_row[:, :], 0.0).then_inc(zeros_ready, 1)
            link(pool.affine_select(out=ident[:, :], in_=ident[:, :], compare_op=ALU.not_equal, fill=1.0,
                                    base=0, pattern=[[-1, P]], channel_multiplier=1))
            pool.memset(ones[:, :], 1.0)
            pool.memset(minus_half[:, :], -0.5)
            for e in range(E):
                pool.memset(rank_desc[:, :, e:e + 1], float(E - e))
            pool.memset(negmaxT[:, :, :].bitcast(f32), 0.0)
            pool.memset(gateT[:, :, :].bitcast(f32), 0.0)
            for k in range(2):
                pool.memset(router_hi0[k][:, 1, :].bitcast(f32), 0.0)
            pool.memset(be_hilo[:, :].bitcast(f32), 0.0).then_inc(consts_ready, 1)

            def low_part(n, part, whole):
                pool.wait_ge(W_hi, n)
                pool.tensor_tensor(part[lo][:, :], whole, part[hi][:, :].bitcast(f32), ALU.subtract).then_inc(W_lo, 1)

            def k_all(b):
                pool.wait_ge(KT_lo, 1)
                pool.wait_ge(masks_ready, 1)
                if b >= 2:
                    pool.wait_ge(e_psum, turn["exp", b - 2, NC4 - 1])
                for part in (hi, lo):
                    pool.tensor_tensor(K_all[part][:, b % 2, :, :],
                                       KT_p[part][:, b, :].bitcast(f32).unsqueeze(1).broadcast_to([P, H, NKEY]),
                                       head_mask[:, :].unsqueeze(2).broadcast_to([P, H, NKEY]), ALU.mult
                                       ).then_inc(K_all_ready, 1)

            for step in steps:
                kind, b, i = step
                n = LNS * b + i
                if kind == "stats":
                    pool.wait_ge(var_ready, turn[step])
                    pool.tensor_scalar(neg_mean[:, n, :], mean_var[:, n, :, 0], -1.0, 0.0, ALU.mult, ALU.add)
                    link(pool.tensor_scalar(var_eps[:, n, :], mean_var[:, n, :, 1], EPS, 1.0, ALU.add, ALU.mult))
                    pool.tensor_tensor(rstd[:, n, :], var_eps[:, n, :], minus_half[:, :], ALU.pow
                                       ).then_inc(rstd_ready, 1)
                    pool.wait_ge(rstd_ready, turn[step])
                    pool.tensor_tensor(neg_mean_rstd[:, n, :], neg_mean[:, n, :], rstd[:, n, :], ALU.mult
                                       ).then_inc(shift_ready, 1)
                if kind == "keys":
                    k_all(b)
                if kind == "Q":
                    pool.wait_ge(xn_dve, turn["norm", b, 0])
                    pool.wait_ge(xn_act, turn["norm", b, 0])
                    pool.wait_ge(ld_q, 64)
                    pool.tensor_tensor(resid[:, b, :, :], resid[:, b, :, :],
                                       bo_all[:, :].unsqueeze(1).broadcast_to([P, J, D]), ALU.add
                                       ).then_inc(xb_ready, 1)
                if kind == "first_weights":
                    pool.wait_ge(be_ready, 1)
                    pool.wait_ge(W_hi, 2)
                    pool.tensor_tensor(router_hilo[0][:, 1, :], Wg_sb[:, :], router_hilo[0][:, 0, :].bitcast(f32),
                                       ALU.subtract).then_inc(W_lo, 1)
                    pool.tensor_tensor(be_lo[:, :], be_sb[:, :], be_hilo[0:1, :].bitcast(f32), ALU.subtract
                                       ).then_inc(be_ready, 1)
                    low_part(3, We_p, flat(We_sb[:, :, :]))
                if kind == "second_weights":
                    low_part(4, w1_p, flat(w1_sb[:, :, :]))
                    low_part(5, w3_p, flat(w3_sb[:, :, :]))
                if kind == "rows":
                    pool.wait_ge(rows_in[b], 64)
                    pool.tensor_tensor(flat(resid[:, b, :, :]), flat(resid[:, b, :, :]), memory_rows[:, b, :],
                                       ALU.add).then_inc(x3_ready, 1)
                if kind == "gate":
                    n = turn[step]
                    pool.wait_ge(gated_ready, n)
                    pool.wait_ge(gb_ready, n)
                    if n > 2:
                        pool.wait_ge(y_psum, n - 2)
                    pool.tensor_tensor(hidden[:, n % 2, :], gated[:, n % 2, :], gate_bc[:, n % 2, :], ALU.mult
                                       ).then_inc(hidden_ready, 1)

        @block.scalar
        def _(act):
            def high_part(part, whole):
                act.activation(part[hi][:, :], whole, ACT.Copy).then_inc(W_hi, 1)

            act.wait_ge(ctxT_psum, 1)
            act.activation(ctxT[:, :, :, :],
                           bank[0][:, 0:B * NKEY].rearrange("p (b k) -> p b k", b=B).unsqueeze(2)
                           .broadcast_to([P, B, H4, NKEY]), ACT.Copy).then_inc(ctxT_ready, 1)

            for step in steps:
                kind, b, i = step
                par = b % 2
                if kind == "first_weights":
                    act.wait_ge(consts_ready, 1)
                    act.activation(ones_r[:, :], ones[:, :], ACT.Copy)
                    act.wait_ge(ld_ffn0, 80)
                    act.activation(be_hilo[0:1, :], be_sb[:, :], ACT.Copy).then_inc(be_ready, 1)
                    act.activation(router_hilo[0][:, 0, :], Wg_sb[:, :], ACT.Copy).then_inc(W_hi, 1)
                    act.activation(router_hi0[0][:, 0, :], Wg_sb[:, :], ACT.Copy).then_inc(W_hi, 1)
                    high_part(We_p, flat(We_sb[:, :, :]))
                    act.wait_ge(wr_psum, 1)
                    act.activation(router_hilo[1][:, 0, :], ps_of(step)[:, 0:E], ACT.Copy)
                    act.activation(router_hi0[1][:, 0, :], ps_of(step)[:, 0:E], ACT.Copy).then_inc(wr_hi, 1)
                if kind == "second_weights":
                    act.wait_ge(ld_w13, 32)
                    high_part(w1_p, flat(w1_sb[:, :, :]))
                    high_part(w3_p, flat(w3_sb[:, :, :]))
                if kind == "keys" and b == 0:
                    act.wait_ge(KT_ready, 1)
                    act.activation(KT_p[hi][:, :, :], KT[:, :, :], ACT.Copy).then_inc(KT_hi, 1)
                if kind == "norm":
                    n = LNS * b + i
                    act.wait_ge(shift_ready, turn["stats", b, i])
                    if xn_read_by(b, i):
                        act.wait_ge(xT_psum, turn[xn_read_by(b, i)])
                    for j in range(NORM_V, J):
                        last = act.activation(xn[:, par, j, :], resid[:, b, j, :], ACT.Identity,
                                              bias=neg_mean_rstd[:, n, j:j + 1], scale=rstd[:, n, j:j + 1])
                    last.then_inc(xn_act, 1)
                if kind == "T":
                    act.wait_ge(xT_psum, turn[step])
                    if i == 3 and b >= 3:
                        act.wait_ge(h3_psum, turn["h3", b - 3, NCH - 1])
                    act.activation(x1T[:, par, :] if i == 0 else split_xT(i, b)[hi], ps_of(step)[:, :], ACT.Copy
                                   ).then_inc(xT_hi, 1)
                if kind == "Q":
                    act.wait_ge(q_psum, turn[step])
                    act.activation(q_p[hi][:, par, :], ps_of(step)[:, :], ACT.Identity, bias=bq_col[:, :]
                                   ).then_inc(q_hi, 1)
                if kind == "maxT":
                    act.wait_ge(nT_psum, turn[step])
                    act.activation(negmaxT[0:H, par, :], ps_of(step)[0:H, :], ACT.Copy).then_inc(nT_ready, 1)
                if kind == "exp":
                    act.wait_ge(e_psum, turn[step])
                    act.activation(probsT[:, par, i, :], ps_of(step)[:, :], ACT.Exp, scale=SCALE
                                   ).then_inc(probs_ready, 1)
                if kind == "attnT":
                    act.wait_ge(aT_psum, turn[step])
                    act.activation(aT[:, par, :], ps_of(step)[:, :], ACT.Copy).then_inc(aT_ready, 1)
                if kind == "route":
                    act.wait_ge(shifted, turn[step])
                    act.activation(rt[i][1][:, :, :], rt[i][0][:, :, :], ACT.Exp).then_inc(exps, 1)
                if kind == "conv":
                    act.wait_ge(convT_psum, turn[step])
                    act.activation(convT[:, par, :, :], ps_of(step)[:, 0:J * COMP], ACT.Copy).then_inc(convT_ready, 1)
                if kind == "gateT":
                    act.wait_ge(gT_psum, turn[step])
                    if b >= 3:
                        act.wait_ge(gb_psum, turn["gate", b - 3, NCH - 1])
                    act.activation(gateT[0:2 * E, b % 3, :], ps_of(step)[0:2 * E, :], ACT.Copy).then_inc(gT_ready, 1)
                if kind == "h3":
                    n = turn[step]
                    act.wait_ge(h1_psum, n)
                    if n > 2:
                        act.wait_ge(gated_ready, n - 2)
                    act.activation(silu_h[:, n % 2, :], ps_h1[:, :], ACT.Silu).then_inc(silu_ready, 1)
                if kind == "gate":
                    n = turn[step]
                    act.wait_ge(gb_psum, n)
                    if n > 2:
                        act.wait_ge(hidden_ready, n - 2)
                    act.activation(gate_bc[:, n % 2, :], ps_gate[:, :], ACT.Copy).then_inc(gb_ready, 1)
                if kind == "out":
                    act.wait_ge(y_psum, turn["y", b, NCH - 1])
                    act.activation(yT, ps_y[:, :], ACT.Copy).then_inc(yT_ready, 1)

        @block.vector
        def _(dve):
            own = [0]

            def link(ins):
                own[0] += 1
                ins.then_inc(dve_step, 1)
                dve.wait_ge(dve_step, own[0])

            dve.wait_ge(consts_ready, 1)
            link(dve.tensor_reduce(head_mask[:, :], ident[:, :].rearrange("p (h k) -> p h k", h=H), AX.X, ALU.add))
            link(dve.tensor_reduce(key_head_mask[:, :], ident[:, :].rearrange("p (h k) -> p h k", h=H4), AX.X, ALU.add))
            dve.tensor_copy(head_rows[:, :, :], ident[:, 0:H].unsqueeze(2).broadcast_to([P, H, NKEY]))
            link(dve.tensor_tensor(expert_mask[:, :], ident[:, 0:E], ident[:, E:2 * E], ALU.add))
            dve.tensor_copy(expert_rows[:, :, :], expert_mask[:, :].unsqueeze(2).broadcast_to([P, E, HID])
                            ).then_inc(masks_ready, 1)
            def keys_and_values():
                dve.wait_ge(kv_psum, 2)
                dve.wait_ge(ld_ctx, 80)
                dve.tensor_scalar(KT[:, :, :].rearrange("p b k -> p (b k)"), bank[1][:, 0:B * NKEY], bk_col[:, :], None,
                                  ALU.add).then_inc(KT_ready, 1)
                dve.wait_ge(KT_hi, 1)
                dve.tensor_tensor(KT_p[lo][:, :, :], KT[:, :, :], KT_p[hi][:, :, :].bitcast(f32), ALU.subtract
                                  ).then_inc(KT_lo, 1)
                v_ps = bank[2][:, :].rearrange("p (b c h k) -> p b c h k", b=B, c=NC4, h=H4)
                for b in range(B):
                    last = dve.tensor_tensor(V_aug[:, b, :, :, 0:DK], v_ps[:, b],
                                             key_head_mask[:, :].unsqueeze(1).unsqueeze(3).broadcast_to([P, NC4, H4, DK]),
                                             ALU.mult)
                last.then_inc(V_ready, 1)
                dve.tensor_copy(V_aug[:, :, :, :, DK:VW].rearrange("p b c h a -> p (b c) (h a)"),
                                key_head_mask[:, :].unsqueeze(1).broadcast_to([P, B * NC4, H4])).then_inc(V_ready, 1)

            def route(step):
                _, b, k = step
                d, ex, l, key, one1, l2, d2, one2, sel = rt[k]
                picked = key
                m1, k1, m2, k2, total, inv = rs[k]
                G = GROUP * J

                def bc(v):
                    return v[:, :].unsqueeze(2).broadcast_to([P, G, E])

                dve.wait_ge(logit_psum, turn[step])
                logits = ps_of(step)[:, 0:G * 2 * E].rearrange("p (j s e) -> p j e s", j=G, s=2)
                dve.tensor_reduce(l[:, :, :], logits, AX.X, ALU.add).then_inc(logit_read, 1)
                if k == 0:
                    dve.wait_ge(logit_read, turn[step])
                    link(dve.tensor_tensor(l[:, :, :], l[:, :, :],
                                           bg_all[:, :].unsqueeze(1).broadcast_to([P, G, E]), ALU.add))
                dve.wait_ge(logit_read, turn[step])
                link(dve.tensor_reduce(m1[:, :], l[:, :, :], AX.X, ALU.max))
                dve.tensor_tensor(d[:, :, :], l[:, :, :], bc(m1), ALU.subtract).then_inc(shifted, 1)
                dve.wait_ge(shifted, turn[step])
                link(dve.scalar_tensor_tensor(flat(key[:, :, :]), flat(d[:, :, :]), 0.0, flat(rank_desc[:, :, :]),
                                              ALU.is_ge, ALU.mult))
                link(dve.tensor_reduce(k1[:, :], key[:, :, :], AX.X, ALU.max))
                link(dve.tensor_tensor(one1[:, :, :], key[:, :, :], bc(k1), ALU.is_equal))
                link(dve.scalar_tensor_tensor(flat(l2[:, :, :]), flat(one1[:, :, :]), -1e38, flat(d[:, :, :]),
                                              ALU.mult, ALU.add))
                link(dve.tensor_reduce(m2[:, :], l2[:, :, :], AX.X, ALU.max))
                link(dve.tensor_tensor(d2[:, :, :], l2[:, :, :], bc(m2), ALU.subtract))
                link(dve.scalar_tensor_tensor(flat(key[:, :, :]), flat(d2[:, :, :]), 0.0, flat(rank_desc[:, :, :]),
                                              ALU.is_ge, ALU.mult))
                link(dve.tensor_reduce(k2[:, :], key[:, :, :], AX.X, ALU.max))
                link(dve.tensor_tensor(one2[:, :, :], key[:, :, :], bc(k2), ALU.is_equal))
                link(dve.tensor_tensor(sel[:, :, :], one1[:, :, :], one2[:, :, :], ALU.add))
                dve.wait_ge(exps, turn[step])
                link(dve.tensor_tensor(picked[:, :, :], ex[:, :, :], sel[:, :, :], ALU.mult))
                link(dve.tensor_reduce(total[:, :], (picked if k == 0 else ex)[:, :, :], AX.X, ALU.add))
                link(dve.reciprocal(inv[:, :], total[:, :]))
                of_pair = gate[:, k, b - GROUP + 1:b + 1, :, :].rearrange("p b j e -> p (b j) e")
                link(dve.tensor_tensor(of_pair, picked[:, :, :], bc(inv), ALU.mult))
                if k == 1:
                    parts = gate_hilo[:, b - GROUP + 1:b + 1, :, :].rearrange("p b j e -> p (b j) e")
                    link(dve.tensor_copy(parts[:, :, 0:E], of_pair))
                    dve.tensor_tensor(parts[:, :, E:2 * E], of_pair, parts[:, :, 0:E].bitcast(f32), ALU.subtract
                                      ).then_inc(gate_ready, 1)

            for step in steps:
                kind, b, i = step
                par = b % 2
                if kind == "keys" and b == 0:
                    keys_and_values()
                if kind == "first_weights":
                    dve.wait_ge(wr_hi, 1)
                    dve.tensor_tensor(router_hilo[1][:, 1, :], ps_of(step)[:, 0:E],
                                      router_hi0[1][:, 0, :].bitcast(f32), ALU.subtract).then_inc(wr_lo, 1)
                if kind == "stats":
                    n = LNS * b + i
                    if i == 0:
                        dve.wait_ge(ld_x[b], 16)
                    if i == 1:
                        dve.wait_ge(x1_ready, turn["O", b, 0])
                    if i == 2:
                        dve.wait_ge(x_read, 2 * turn["X", b, 3])
                    if i == 3:
                        dve.wait_ge(x3_ready, turn["rows", b, 0])
                    for j in range(J):
                        last = dve.bn_stats(bn[:, n, j, :], resid[:, b, j, :])
                    link(last)
                    for j in range(J):
                        last = dve.bn_aggr(mean_var[:, n, j, :], bn[:, n, j, :])
                    last.then_inc(var_ready, 1)
                if kind == "norm":
                    n = LNS * b + i
                    dve.wait_ge(rstd_ready, turn["stats", b, i])
                    if xn_read_by(b, i):
                        dve.wait_ge(xT_psum, turn[xn_read_by(b, i)])
                    for j in range(NORM_V):
                        last = dve.tensor_scalar(xn[:, par, j, :], resid[:, b, j, :], mean_var[:, n, j, 0:1],
                                                 rstd[:, n, j:j + 1], ALU.subtract, ALU.mult)
                    last.then_inc(xn_dve, 1)
                if kind == "T" and i > 0:
                    dve.wait_ge(xT_hi, turn[step])
                    dve.tensor_tensor(split_xT(i, b)[lo], ps_of(step)[:, :], split_xT(i, b)[hi].bitcast(f32),
                                      ALU.subtract).then_inc(xT_lo, 1)
                if kind == "Q":
                    dve.wait_ge(q_hi, turn[step])
                    dve.scalar_tensor_tensor(q_p[lo][:, par, :], ps_of(step)[:, :], bq_col[:, :],
                                             q_p[hi][:, par, :].bitcast(f32), ALU.add, ALU.subtract).then_inc(q_lo, 1)
                if kind == "max":
                    dve.wait_ge(m_psum, turn[step])
                    dve.tensor_reduce(negmax[:, par, i, :], ps_of(step)[:, :].rearrange("p (h k) -> p h k", h=H),
                                      AX.X, ALU.max, negate=True).then_inc(negmax_ready, 1)
                if kind == "V":
                    ps = ps_of(step)[:, 0:2 * H * VW].rearrange("p (h v) -> p h v", v=VW)
                    dve.wait_ge(pv_psum, turn[step])
                    link(dve.reciprocal(rden[:, 2 * par + i, :], ps[:, :, DK]))
                    dve.tensor_tensor(attn[:, par, 2 * i:2 * i + 2, :, :].rearrange("p j h k -> p (j h) k"),
                                      ps[:, :, 0:DK], rden[:, 2 * par + i, :].unsqueeze(2).broadcast_to([P, 2 * H, DK]),
                                      ALU.mult).then_inc(attn_ready, 1)
                if kind == "O":
                    dve.wait_ge(o_psum, turn[step])
                    dve.wait_ge(xb_ready, turn["Q", b, 0])
                    dve.tensor_tensor(flat(resid[:, b, :, :]), ps_of(step)[:, :], flat(resid[:, b, :, :]), ALU.add
                                      ).then_inc(x1_ready, 1)
                if kind == "route":
                    if b == GROUP - 1 and i == 0:
                        dve.wait_ge(ld_ffn0, 80)
                    route(step)
                if kind == "X":
                    dve.wait_ge(x_psum, turn[step])
                    jj, g = i // 2, i % 2
                    for e in range(E // 2):
                        for u in range(2):
                            j = 2 * jj + u
                            ins = dve.scalar_tensor_tensor(resid[:, b, j, :], ps_of(step, u)[:, D * e:D * e + D],
                                                           gate[:, 0, b, j, E // 2 * g + e:E // 2 * g + e + 1],
                                                           resid[:, b, j, :], ALU.mult, ALU.add)
                            if e == E // 2 - 1:
                                ins.then_inc(x_read, 1)
                            else:
                                own[0] += 1
                                ins.then_inc(dve_step, 1)
                            if not (e == E // 2 - 1 and u == 1):
                                if e or u:
                                    dve.wait_ge(dve_step, own[0] - (1 if e < E // 2 - 1 else 0))
                    dve.wait_ge(x_read, 2 * turn[step])
                if kind == "conv":
                    dve.wait_ge(comp_psum, turn[step])
                    if b < 2:
                        dve.wait_ge(ld_conv, 32)
                    else:
                        dve.wait_ge(rows_in[b - 2], 64)
                    dve.tensor_tensor(comp[:, par, :], ps_of(step, 1)[0:COMP, 0:D], convb_all[:, :], ALU.add
                                      ).then_inc(comp_ready, 1)
                if kind == "gate":
                    n = turn[step]
                    dve.wait_ge(silu_ready, n)
                    dve.wait_ge(h3_psum, n)
                    if n > 2:
                        dve.wait_ge(hidden_ready, n - 2)
                    dve.tensor_tensor(gated[:, n % 2, :], ps_h3[n % 2][:, :], silu_h[:, n % 2, :], ALU.mult
                                      ).then_inc(gated_ready, 1)
                if kind == "out":
                    dve.wait_ge(yt_psum, b + 1)
                    dve.tensor_tensor(flat(resid[:, b, :, :]), ps_of(step)[:, :], flat(resid[:, b, :, :]), ALU.add
                                      ).then_inc(x4_ready, 1)

        @block.tensor
        def _(pe):
            last_reader = {}

            def take(step, reader, count, i=0):
                k = bank_of[(*step, i)]
                if k in last_reader:
                    pe.wait_ge(*last_reader[k])
                last_reader[k] = (reader, count)
                return bank[k]

            def take_over(k):
                if k in last_reader:
                    pe.wait_ge(*last_reader.pop(k))

            def three_passes(o, lhs, rhs, start=True, stop=True):
                pe.matmul(o, lhs[hi], rhs[hi], start=start, stop=False)
                pe.matmul(o, lhs[lo], rhs[hi], start=False, stop=False)
                return pe.matmul(o, lhs[hi], rhs[lo], start=False, stop=stop)

            pe.wait_ge(consts_ready, 1)
            pe.wait_ge(ld_ctx, 80)
            ps = take(("setup", 0, 0), ctxT_ready, 1, 0)
            pe.transpose(ps[:, 0:P], ctx_sb[:, :], ident[:, :]).then_inc(ctxT_psum, 1)
            pe.wait_ge(ctxT_ready, 1)
            ps = take(("setup", 0, 0), KT_ready, 1, 1)
            pe.matmul(ps[:, 0:P], Wk_sb[:, :], ctxT[:, :, 0, :], start=True, stop=True).then_inc(kv_psum, 1)
            ps = take(("setup", 0, 0), V_ready, 2, 2)
            for b in range(B):
                pe.matmul(ps[:, D * b:D * b + D], ctxT[:, b, :, :].rearrange("p h k -> p (h k)"), Wv_sb[:, :],
                          start=True, stop=False)
                last = pe.matmul(ps[:, D * b:D * b + D], ones[:, :], bv_row[:, :], start=False, stop=True)
            last.then_inc(kv_psum, 1)

            for step in steps:
                kind, b, i = step
                par = b % 2
                n = turn[step]
                if kind == "T":
                    ps = take(step, xT_hi if i == 0 else xT_lo,
                              n if i == 0 else xT_splits(b, i))
                    pe.wait_ge(xn_dve, turn["norm", b, i])
                    pe.wait_ge(xn_act, turn["norm", b, i])
                    for j in range(J):
                        last = pe.transpose(ps[:, P * j:P * j + P], xn[:, par, j, :], ident[:, :])
                    last.then_inc(xT_psum, 1)
                if kind == "first_weights":
                    ps = take(step, wr_lo, 1)
                    pe.wait_ge(ld_ffn0, 80)
                    pe.transpose(ps[:, 0:E], wr_sb[:, :], ident[0:E, 0:E]).then_inc(wr_psum, 1)
                if kind == "Q":
                    ps = take(step, q_lo, n)
                    pe.wait_ge(ld_q, 64)
                    pe.wait_ge(xT_hi, turn["T", b, 0])
                    pe.matmul(ps[:, :], Wq_sb[:, :], x1T[:, par, :], start=True, stop=True).then_inc(q_psum, 1)
                if kind == "max":
                    ps = take(step, negmax_ready, n)
                    pe.wait_ge(q_hi, turn["Q", b, 0])
                    pe.wait_ge(K_all_ready, 2 * turn["keys", b, 0])
                    pe.matmul(ps[:, :], q_p[hi][:, par, P * i:P * i + P], flat(K_all[hi][:, par, :, :]),
                              start=True, stop=True).then_inc(m_psum, 1)
                if kind == "maxT":
                    ps = take(step, nT_ready, n)
                    pe.wait_ge(negmax_ready, turn["max", b, J - 1])
                    for j in range(J):
                        last = pe.transpose(ps[0:H, P * j:P * j + P], negmax[:, par, j, :], ident[:, :])
                    last.then_inc(nT_psum, 1)
                if kind == "exp":
                    ps = take(step, probs_ready, n)
                    pe.wait_ge(nT_ready, turn["maxT", b, 0])
                    pe.wait_ge(q_lo, turn["Q", b, 0])
                    three_passes(ps[:, :], [flat(w[:, par, H4 * i:H4 * i + H4, :]) for w in K_all],
                                 [q[:, par, :] for q in q_p], stop=False)
                    pe.matmul(ps[:, :], flat(head_rows[:, H4 * i:H4 * i + H4, :]), negmaxT[:, par, :],
                              start=False, stop=True).then_inc(e_psum, 1)
                if kind == "V":
                    ps = take(step, attn_ready, n)
                    pe.wait_ge(probs_ready, turn["exp", b, NC4 - 1])
                    pe.wait_ge(V_ready, 2)
                    for u in range(2):
                        j = 2 * i + u
                        for c in range(NC4):
                            at = u * H * VW + c * H4 * VW
                            last = pe.matmul(ps[:, at:at + H4 * VW], probsT[:, par, c, P * j:P * j + P],
                                             flat(V_aug[:, b, c, :, :]), start=True, stop=True)
                    last.then_inc(pv_psum, 1)
                if kind == "attnT":
                    ps = take(step, aT_ready, n)
                    pe.wait_ge(attn_ready, turn["V", b, 1])
                    for j in range(J):
                        last = pe.transpose(ps[:, P * j:P * j + P], flat(attn[:, par, j, :, :]), ident[:, :])
                    last.then_inc(aT_psum, 1)
                if kind == "O":
                    ps = take(step, x1_ready, n)
                    pe.wait_ge(aT_ready, turn["attnT", b, 0])
                    for j in range(J):
                        last = pe.matmul(ps[:, D * j:D * j + D], aT[:, par, P * j:P * j + P], Wo_sb[:, :],
                                         start=True, stop=True)
                    last.then_inc(o_psum, 1)
                if kind == "route":
                    ln = 1 if i == 0 else 3
                    ps = take(step, logit_read, n)
                    pe.wait_ge(xT_lo, xT_splits(b, ln))
                    if i == 0:
                        pe.wait_ge(W_lo, 1)
                    else:
                        pe.wait_ge(wr_lo, 1)
                    for u in range(GROUP * J):
                        x_hi, x_lo = [a[:, P * (u % J):P * (u % J) + P] for a in split_xT(ln, b - GROUP + 1 + u // J)]
                        o = ps[:, 2 * E * u:2 * E * u + 2 * E]
                        pe.matmul(o, x_hi, flat(router_hilo[i][:, :, :]), start=True, stop=False)
                        last = pe.matmul(o, x_lo, flat(router_hi0[i][:, :, :]), start=False, stop=True)
                    last.then_inc(logit_psum, 1)
                if kind == "X":
                    cols = slice(D * E // 2 * (i % 2), D * E // 2 * (i % 2 + 1))
                    pe.wait_ge(W_lo, 2)
                    pe.wait_ge(be_moved, 16)
                    for u in range(2):
                        j = 2 * (i // 2) + u
                        ps = take(step, x_read, 2 * (n - 1) + u + 1, u)
                        three_passes(ps[:, :], [a[:, P * j:P * j + P] for a in split_xT(1, b)],
                                     [w[:, cols] for w in We_p], stop=False)
                        last = pe.matmul(ps[:, :], ones_r[:, :], be_hilo[:, cols], start=False, stop=True)
                    last.then_inc(x_psum, 1)
                if kind == "conv":
                    ps = take(step, convT_ready, n)
                    pe.wait_ge(xn_dve, turn["norm", b, 2])
                    pe.wait_ge(xn_act, turn["norm", b, 2])
                    at = HALF // J
                    for j in range(J):
                        last = pe.transpose(ps[:, COMP * j:COMP * j + COMP], xn[at:at + COMP, par, j, :],
                                            ident[at:at + COMP, at:at + COMP])
                    last.then_inc(convT_psum, 1)
                    ps = take(step, comp_ready, n, 1)
                    pe.wait_ge(convT_ready, n)
                    pe.wait_ge(ld_conv, 32)
                    for j in range(J):
                        last = pe.matmul(ps[0:COMP, 0:D], convT[:, par, j, :], conv_sb[:, j, :],
                                         start=(j == 0), stop=(j == J - 1))
                    last.then_inc(comp_psum, 1)
                if kind == "gateT":
                    ps = take(step, gT_ready, n)
                    pe.wait_ge(gate_ready, b // GROUP + 1)
                    for j in range(J):
                        last = pe.transpose(ps[0:2 * E, P * j:P * j + P], gate_hilo[:, b, j, :].bitcast(f32), ident[:, :])
                    last.then_inc(gT_psum, 1)
                cols = slice(P * i, P * i + P)
                if kind == "h1":
                    if n == 1:
                        take_over(H1_BANK)
                    pe.wait_ge(W_lo, 4)
                    pe.wait_ge(xT_lo, xT_splits(b, 3))
                    if n > 1:
                        pe.wait_ge(silu_ready, n - 1)
                    three_passes(ps_h1[:, :], [w[:, cols] for w in w1_p], split_xT(3, b)).then_inc(h1_psum, 1)
                if kind == "h3":
                    if n <= 2:
                        take_over(H3_BANKS[n % 2])
                    if n > 2:
                        pe.wait_ge(gated_ready, n - 2)
                    three_passes(ps_h3[n % 2][:, :], [w[:, cols] for w in w3_p], split_xT(3, b)).then_inc(h3_psum, 1)
                if kind == "gate":
                    if n == 1:
                        take_over(GATE_BANK)
                    pe.wait_ge(gT_ready, turn["gateT", b, 0])
                    pe.wait_ge(masks_ready, 1)
                    if n > 1:
                        pe.wait_ge(gb_ready, n - 1)
                    pe.matmul(ps_gate[:, :], flat(expert_rows[:, :, :])[:, cols], gateT[:, b % 3, :],
                              start=True, stop=True).then_inc(gb_psum, 1)
                if kind == "y":
                    if n == 1:
                        take_over(Y_BANK)
                    pe.wait_ge(ld_w2, 16)
                    pe.wait_ge(hidden_ready, n)
                    if i == 0 and b >= 1:
                        pe.wait_ge(yT_ready, b)
                    pe.matmul(ps_y[:, :], w2_sb[:, i, :], hidden[:, n % 2, :], start=(i == 0), stop=(i == NCH - 1)
                              ).then_inc(y_psum, 1)
                if kind == "out":
                    pe.wait_ge(yT_ready, b + 1)
                    ps = take(step, x4_ready, b + 1)
                    for j in range(J):
                        last = pe.transpose(ps[:, P * j:P * j + P], yT[:, P * j:P * j + P], ident[:, :])
                    last.then_inc(yt_psum, 1)


_INS = ['x', 'ctx_1024', 'L0_xattn_Wq', 'L0_xattn_bq', 'L0_xattn_Wk', 'L0_xattn_bk', 'L0_xattn_Wv', 'L0_xattn_bv',
        'L0_xattn_Wo', 'L0_xattn_bo', 'L0_ffn_We', 'L0_ffn_be', 'L0_ffn_Wg', 'L0_ffn_bg', 'L1_xattn_conv_w',
        'L1_xattn_conv_b', 'L1_ffn_w_router', 'L1_ffn_w1', 'L1_ffn_w2', 'L1_ffn_w3']
_OUTS = [((4, 512, 128), 'float32')]


def kernel(**inputs):
    import numpy as _np
    import concourse.bacc as _bacc
    from concourse import mybir as _mybir
    from concourse.bass_utils import run_bass_kernel_spmd as _run

    nc = _bacc.Bacc("TRN2", target_bir_lowering=False, num_devices=1)
    arrays, args = {}, []
    for name in _INS:
        a = _np.ascontiguousarray(inputs[name])
        arrays[f"in_{name}_dram"] = a
        args.append(nc.dram_tensor(f"in_{name}_dram", a.shape, _mybir.dt.from_np(a.dtype), kind="ExternalInput").ap())
    for i, (shape, dtype) in enumerate(_OUTS):
        dt = _mybir.dt.from_np(_np.dtype(dtype))
        args.append(nc.dram_tensor(f"out_{i}_dram", shape, dt, kind="ExternalOutput").ap())
    block_program(nc, *args)
    r = _run(nc, [arrays], core_ids=[0])
    got = tuple(r.results[0][f"out_{i}_dram"] for i in range(len(_OUTS)))
    return got[0]
```

```python
import concourse.bass as bass
from concourse import mybir
from contextlib import ExitStack



def order_of_steps(batches, chunks):
    slots = 4
    prepare = ([("stats", 0), ("norm", 0), ("keys", 0), ("T", 0), ("Q", 0)] + [("max", j) for j in range(slots)]
               + [("maxT", 0)] + [("exp", c) for c in range(slots)] + [("V", 0), ("V", 1), ("attnT", 0), ("O", 0)]
               + [("stats", 1), ("norm", 1), ("T", 1), ("route", 0), ("pick", 0), ("weigh", 0)] + [("X", i) for i in range(slots)]
               + [("stats", 2), ("norm", 2), ("conv", 0), ("rows", 0)]
               + [("stats", 3), ("norm", 3), ("T", 3), ("route", 1), ("pick", 1), ("weigh", 1), ("gateT", 0)])
    every, each_chunk = range(batches), range(chunks)
    rows = {
        "w": [(kind, 0, 0) for kind in ("values", "first_weights", "second_weights", "third_weights")],
        "h": [(kind, b, c) for b in every for c in each_chunk for kind in ("h1", "h3", "gate")],
        "s": [("split", b, c) for b in every for c in each_chunk],
        "y": [(kind, b, c) for b in every for kind, c in [("y", c) for c in each_chunk] + [("out", 0)]],
    }
    rows.update({"abcd"[b]: [(kind, b, i) for kind, i in prepare] for b in every})
    next_of = {letter: iter(row) for letter, row in rows.items()}
    steps = [next(next_of[letter]) for letter in "".join(TURNS)]
    assert len(steps) == sum(len(row) for row in rows.values())
    return steps


TURNS = (
    "aaaaaabaababwbabacbabaabbawbababaabbabbabwaaaaacbbaabbacbwbabbaabbabaabahbahabacshhhbhchchshchbhhhcs"
    "hcbyyhhhsbhcdhyhccchscbbdcycdbdhscdchychbhdhcdddcsyhhhsdcdhccsdhydhydcyhhcdhdcsdshhyhddschyhhhhysdhc"
    "hydyshhcdyhhdcshdshcydcyhhsdhhhchdchyhshshhccyshchhysdhhychyshhhhhhsdyhhyhysdhhhdsyhsdhhsyhdhhyhshhd"
    "syhhdhyshdhddhshyhyhydhhhhshhyhshyshshhyhsyhhhhyhshyhhshhyshyhhhyshyhshhyhhshshsyyyy")


def block_program(nc, x, ctx_1024, Wq, bq, Wk, bk, Wv, bv, Wo, bo, We, be, Wg, bg, conv_w, conv_b,
                  w_router, w1, w2, w3, out):
    f32 = mybir.dt.float32
    f32r = mybir.dt.float32r
    ALU = mybir.AluOpType
    ACT = mybir.ActivationFunctionType
    AX = mybir.AxisListType

    B, S, D = x.shape
    NKEY = ctx_1024.shape[1]
    H = 16
    DK = D // H
    E = We.shape[0]
    HID = w1.shape[2]
    P = 128
    J = S // P
    NC4 = H * NKEY // P
    H4 = H // NC4
    EH = E * HID
    NCH = EH // P
    VW = DK + 1
    CONV = conv_w.shape[0]
    HALF = S // 2
    COMP = NKEY // CONV
    EPS = 1e-5
    SCALE = float(DK) ** -0.5
    LNS = 4
    assert CONV == J and D == P

    steps = order_of_steps(B, NCH)

    NBANKS, NSHARED = 8, 3
    uses = {"values": 1, "T": 1, "Q": 1, "max": 1, "maxT": 1, "exp": 1, "V": 1, "attnT": 1, "O": 1, "route": 1, "X": 2,
            "conv": 2, "gateT": 1, "out": 1, "first_weights": 1}
    SETUP_USES = 2
    bank_of = {("setup", 0, 0, i): i for i in range(SETUP_USES)}
    n = SETUP_USES
    gated_from = next(i for i, step in enumerate(steps) if step[0] == "h1")
    for at, step in enumerate(steps):
        for i in range(uses.get(step[0], 0)):
            bank_of[(*step, i)] = n % (NBANKS if at < gated_from else NSHARED)
            n += 1

    splits = [step for step in steps if step[0] == "T" and step[2] > 0]
    split_turn = {step: n + 1 for n, step in enumerate(splits)}
    halves = [[step for step in steps if step[0] == "X" and step[2] % 2 == half] for half in range(2)]
    half_turn = {step: n + 1 for half in halves for n, step in enumerate(half)}

    turn, come = {}, {}
    for step in steps:
        come[step[0]] = turn[step] = come.get(step[0], 0) + 1

    es = ExitStack()
    with es:
        def sb(name, shape, dt=f32):
            return es.enter_context(nc.sbuf_tensor(name, shape, dt))

        def sem(name):
            return es.enter_context(nc.semaphore(name))

        ident = sb("ident", [P, P])
        ones = sb("ones", [P, P])
        minus_half = sb("minus_half", [P, J])
        rank_desc = sb("rank_desc", [P, J, E])
        head_mask = sb("head_mask", [P, H])
        key_head_mask = sb("key_head_mask", [P, H4])
        head_rows = sb("head_rows", [P, H, NKEY], f32r)
        expert_mask = sb("expert_mask", [P, E])
        expert_rows = sb("expert_rows", [P, E, HID], f32r)
        ones_r = sb("ones_r", [P, P], f32r)

        ctx_sb = sb("ctx_sb", [P, D])
        ctxT = sb("ctxT", [P, B, H4, NKEY])
        Wk_sb = sb("Wk_sb", [P, D])
        Wv_sb = sb("Wv_sb", [P, D])
        Wq_sb = sb("Wq_sb", [P, D])
        Wo_sb = sb("Wo_sb", [P, D])
        bk_col = sb("bk_col", [P, 1])
        bq_col = sb("bq_col", [P, 1])
        bv_row = sb("bv_row", [P, D])
        bo_all = sb("bo_all", [P, D])
        bg_all = sb("bg_all", [P, E])
        convb_all = sb("convb_all", [COMP, D])
        We_sb = sb("We_sb", [P, E, D])
        Wg_sb = sb("Wg_sb", [P, E])
        conv_sb = sb("conv_sb", [P, CONV, D])
        wr_sb = sb("wr_sb", [E, D])
        router_hilo = [sb(f"router{k}_hilo", [P, 2, E], f32r) for k in range(2)]
        router_hi0 = [sb(f"router{k}_hi0", [P, 2, E], f32r) for k in range(2)]
        We_p = [sb(f"We_{s}", [P, E * D], f32r) for s in ("hi", "lo")]
        w1_p = [sb(f"w1_{s}", [P, EH], f32r) for s in ("hi", "lo")]
        w3_p = [sb(f"w3_{s}", [P, EH], f32r) for s in ("hi", "lo")]
        w2_p = [sb(f"w2_{s}", [P, NCH * D], f32r) for s in ("hi", "lo")]
        w1_sb, w3_sb = sb("w1_sb", [P, EH]), sb("w3_sb", [P, EH])
        w2_sb = w1_sb
        be_hilo = sb("be_hilo", [P, E * D], f32r)
        KT = sb("KT", [P, B, NKEY])
        KT_p = [sb(f"KT_{s}", [P, B, NKEY], f32r) for s in ("hi", "lo")]
        K_all = [sb(f"K_all_{s}", [P, 2, H, NKEY], f32r) for s in ("hi", "lo")]
        V_aug = sb("V_aug", [P, B, NC4, H4, VW])

        resid = sb("resid", [P, B, J, D])
        memory_rows = sb("memory_rows", [P, B, J * D])
        bn = sb("bn", [P, LNS * B, J, 6])
        mean_var = sb("mean_var", [P, LNS * B, J, 2])
        var_eps = sb("var_eps", [P, LNS * B, J])
        rstd = sb("rstd", [P, LNS * B, J])
        neg_mean_rstd = sb("neg_mean_rstd", [P, LNS * B, J])
        xn = sb("xn", [P, 3, J, D])
        x1T = sb("x1T", [P, S])
        xT_p = [sb(f"xT_{s}", [P, 2, S], f32r) for s in ("hi", "lo")]
        x4T_p = [sb(f"x4T_{s}", [P, 3, S], f32r) for s in ("hi", "lo")]
        q_p = [sb(f"q_{s}", [P, 2, S], f32r) for s in ("hi", "lo")]
        negmax = sb("negmax", [P, 2, J, H])
        negmaxT = sb("negmaxT", [P, 2, S], f32r)
        probsT = sb("probsT", [P, 2, NC4, S])
        rden = sb("rden", [P, 4, 2 * H])
        attn = sb("attn", [P, 2, J, H, DK])
        aT = sb("aT", [P, 2, S])
        rt = [[sb(f"rt{k}_{i}", [P, J, E]) for i in range(9)] for k in range(2)]
        rs = [[sb(f"rs{k}_{i}", [P, J]) for i in range(6)] for k in range(2)]
        gate = sb("gate", [P, 2, B, J, E])
        gate_hilo = sb("gate_hilo", [P, B, J, 2 * E], f32r)
        gateT = sb("gateT", [P, 3, S], f32r)
        convT = sb("convT", [P, 2, J, COMP])
        comp = sb("comp", [COMP, 2, D])
        silu_h = sb("silu_h", [P, 2, S])
        gated = sb("gated", [P, 2, S])
        hidden = sb("hidden", [P, 2, S])
        hidden_p = [sb(f"hidden_{s}", [P, 2, S], f32r) for s in ("hi", "lo")]
        be_sb = hidden[0:1, :, :].rearrange("p s n -> p (s n)")
        be_lo = hidden_p[1][0:1, :, :].rearrange("p s n -> p (s n)")
        assert E * D == 2 * S
        yT = sb("yT", [P, S])
        weighted = We_sb[:, :, :].rearrange("p (u e) o -> p u e o", u=2)

        bank = [es.enter_context(nc.psum_tensor(f"bank{i}", [P, S], f32)) for i in range(NBANKS)]
        H1_BANK, H3_BANKS, GATE_BANK, Y_BANK = 3, (4, 5), 6, 7
        ps_h1, ps_gate, ps_y = bank[H1_BANK], bank[GATE_BANK], bank[Y_BANK]
        ps_h3 = [bank[k] for k in H3_BANKS]

        ld_ctx, ld_q, ld_v, ld_o, ld_ffn0, ld_conv, ld_w13, ld_w2 = (sem(s) for s in (
            "ld_ctx", "ld_q", "ld_v", "ld_o", "ld_ffn0", "ld_conv", "ld_w13", "ld_w2"))
        ld_x = [sem(f"ld_x{b}") for b in range(B)]
        be_moved = sem("be_moved")
        ident_ready, zeros_ready, consts_ready, gateT_zeroed, masks_ready, rows_ready = (sem(s) for s in (
            "ident_ready", "zeros_ready", "consts_ready", "gateT_zeroed_s", "masks_ready", "rows_ready"))
        ctxT_psum, ctxT_ready, kv_psum, KT_ready, KT_hi, KT_lo, K_all_ready, V_ready = (sem(s) for s in (
            "ctxT_psum", "ctxT_ready", "kv_psum", "KT_ready", "KT_hi_s", "KT_lo_s", "K_all_ready", "V_ready"))
        wr_psum, wr_hi, wr_lo = sem("wr_psum"), sem("wr_hi"), sem("wr_lo")
        W_hi, W_lo, be_ready = sem("W_hi"), sem("W_lo"), sem("be_ready")
        var_ready, rstd_ready, shift_ready, xn_dve, xn_act = (sem(s) for s in (
            "var_ready", "rstd_ready", "shift_ready", "xn_dve", "xn_act"))
        xT_psum, xT_hi, xT_lo = sem("xT_psum"), sem("xT_hi_s"), sem("xT_lo_s")
        q_psum, q_hi, q_lo, m_psum, negmax_ready, nT_psum, nT_ready, e_psum, probs_ready, pv_psum, attn_ready = (
            sem(s) for s in ("q_psum", "q_hi_s", "q_lo_s", "m_psum", "negmax_ready", "nT_psum", "nT_ready", "e_psum",
                             "probs_ready", "pv_psum", "attn_ready"))
        aT_psum, aT_ready, o_psum, xb_ready, x1_ready = (sem(s) for s in (
            "aT_psum", "aT_ready", "o_psum", "xb_ready", "x1_ready"))
        logit_psum = sem("logit_psum")
        logit_read = sem("logit_read")
        shifted = sem("shifted")
        exps = sem("exps")
        x_psum, x_read, x_weighted, x_paired, x2_ready = (sem(s) for s in (
            "x_psum", "x_read", "x_weighted", "x_paired", "x2_ready"))
        convT_psum, convT_ready, comp_psum, comp_ready, x3_ready = (sem(s) for s in (
            "convT_psum", "convT_ready", "comp_psum", "comp_ready", "x3_ready"))
        rows_in = [sem(f"rows_in{b}") for b in range(B)]
        gate_ready, gT_psum, gT_ready = sem("gate_ready"), sem("gT_psum"), sem("gT_ready")
        h1_psum, h3_psum, gb_psum, silu_ready, gated_ready, hidden_ready, hidden_hi, hidden_lo = (sem(s) for s in (
            "h1_psum", "h3_psum", "gb_psum", "silu_ready", "gated_ready", "hidden_ready", "hidden_hi_s",
            "hidden_lo_s"))
        y_psum, yT_ready, yt_psum, x4_ready, stored = (sem(s) for s in (
            "y_psum", "yT_ready", "yt_psum", "x4_ready", "stored"))
        dve_step, pool_step = sem("dve_step"), sem("pool_step")

        hi, lo = 0, 1
        NORM_V = J // 2

        def split_xT(k, b):
            if k == 3:
                return [x4T_p[s][:, b % 3, :] for s in (hi, lo)]
            return [xT_p[s][:, b % 2, :] for s in (hi, lo)]

        def first_ln_before(b):
            before = [t[1] for t in steps[:steps.index(("norm", b, 0))] if t[0] == "norm" and t[2] == 0]
            return before[-1] if before else None

        def xn_slot(b, k):
            return 2 if k == 0 else b % 2

        def xn_read_by(b, k):
            if k == 0:
                return ("T", first_ln_before(b), 0) if first_ln_before(b) is not None else None
            if k == 1:
                return ("T", b - 2, 3) if b >= 2 else None
            return ("T", b, 1) if k == 2 else None

        def xT_splits(b, k):
            return split_turn["T", b, k]

        def x_turn(step):
            return half_turn[step]

        def ps_of(step, i=0):
            return bank[bank_of[(*step, i)]]

        def flat(v):
            names = " ".join("abcd"[:len(v.shape) - 1])
            return v.rearrange(f"p {names} -> p ({names})")

        block = es.enter_context(nc.Block())

        @block.sync
        def _(sp):
            x_v = x.rearrange("b (p j) d -> b p (j d)", j=J)
            out_v = out.rearrange("b (p j) d -> b p (j d)", j=J)
            resid_v = resid[:, :, :, :].rearrange("p b j d -> p b (j d)")

            def column(v):
                return v.rearrange("(p a) -> p a", a=1)

            def row(v):
                return v.rearrange("(a n) -> a n", a=1)

            sp.dma_start(resid_v[:, 0, :], x_v[0]).then_inc(ld_x[0], 16)
            sp.dma_start(ctx_sb[:, :], ctx_1024.rearrange("b k d -> (b k) d")).then_inc(ld_ctx, 16)
            sp.dma_start(Wk_sb[:, :], Wk).then_inc(ld_ctx, 16)
            sp.dma_start(bk_col[:, :], column(bk)).then_inc(ld_ctx, 16)
            sp.dma_start(resid_v[:, 1, :], x_v[1]).then_inc(ld_x[1], 16)
            sp.dma_start(Wq_sb[:, :], Wq).then_inc(ld_q, 16)
            sp.dma_start(bq_col[:, :], column(bq)).then_inc(ld_q, 16)
            sp.dma_start(Wv_sb[:, :], Wv).then_inc(ld_v, 16)
            sp.wait_ge(zeros_ready, 1)
            sp.dma_start(bv_row[0:1, :], row(bv)).then_inc(ld_v, 16)
            sp.dma_start(Wo_sb[:, :], Wo).then_inc(ld_o, 16)
            sp.dma_start(bo_all[:, :], bo.partition_broadcast(P)).then_inc(ld_o, 16)
            sp.dma_start(We_sb[:, :, :], We.rearrange("e d o -> d e o")).then_inc(ld_ffn0, 16)
            sp.dma_start(Wg_sb[:, :], Wg).then_inc(ld_ffn0, 16)
            sp.dma_start(bg_all[:, :], bg.partition_broadcast(P)).then_inc(ld_ffn0, 16)
            sp.dma_start(be_sb, be.rearrange("(a e) o -> a (e o)", a=1)).then_inc(ld_ffn0, 16)
            sp.dma_start(wr_sb[:, :], w_router).then_inc(ld_ffn0, 16)
            sp.dma_start(conv_sb[:, :, :], conv_w.rearrange("r i o -> i r o")).then_inc(ld_conv, 16)
            sp.dma_start(convb_all[:, :], conv_b.partition_broadcast(COMP)).then_inc(ld_conv, 16)
            for b in range(B):
                sp.dma_start(memory_rows[P - NKEY // J:P, b, :],
                             ctx_1024[b].rearrange("(p j) d -> p (j d)", j=J)).then_inc(rows_in[b], 16)
            sp.dma_start(w1_sb[:, :].rearrange("p (e h) -> p e h", e=E), w1.rearrange("e d h -> d e h")).then_inc(ld_w13, 16)
            sp.dma_start(w3_sb[:, :].rearrange("p (e h) -> p e h", e=E), w3.rearrange("e d h -> d e h")).then_inc(ld_w13, 16)
            for b in range(2, B):
                sp.dma_start(resid_v[:, b, :], x_v[b]).then_inc(ld_x[b], 16)
            sp.wait_ge(be_ready, 2)
            sp.dma_start(be_hilo[1:2, :].bitcast(f32), be_lo.bitcast(f32)).then_inc(be_moved, 16)
            for step in steps:
                kind, b, i = step
                if kind == "third_weights":
                    sp.wait_ge(W_lo, 3)
                    sp.dma_start(w2_sb[:, :].rearrange("p (c d) -> p c d", c=NCH),
                                 w2.rearrange("e h d -> (e h) d").rearrange("(c p) d -> p c d", p=P)
                                 ).then_inc(ld_w2, 16)
                if kind == "rows":
                    sp.wait_ge(xn_dve, turn["norm", b, 2])
                    sp.wait_ge(xn_act, turn["norm", b, 2])
                    src = flat(xn[:, b % 2, :, :])
                    up, mid, old = COMP // J, HALF // J, NKEY // J
                    sp.dma_start(memory_rows[0:mid - up, b, :], src[up:mid, :]).then_inc(rows_in[b], 16)
                    sp.dma_start(memory_rows[mid:P - old, b, :], src[mid + old:P, :]).then_inc(rows_in[b], 16)
                    sp.wait_ge(comp_ready, turn["conv", b, 0])
                    sp.dma_start(memory_rows[mid - up:mid, b, :], comp[:, b % 2, :]).then_inc(rows_in[b], 16)
                if kind == "out":
                    sp.wait_ge(x4_ready, b + 1)
                    sp.dma_start(out_v[b], resid_v[:, b, :]).then_inc(stored, 16)
            sp.wait_ge(stored, 16 * B)

        @block.gpsimd
        def _(pool):
            own = [0]

            def link(ins):
                own[0] += 1
                ins.then_inc(pool_step, 1)
                pool.wait_ge(pool_step, own[0])

            link(pool.memset(ident[:, :], 0.0))
            pool.memset(bv_row[:, :], 0.0).then_inc(zeros_ready, 1)
            link(pool.affine_select(out=ident[:, :], in_=ident[:, :], compare_op=ALU.not_equal, fill=1.0,
                                    base=0, pattern=[[-1, P]], channel_multiplier=1))
            pool.memset(ones[:, :], 1.0).then_inc(ident_ready, 1)
            pool.memset(minus_half[:, :], -0.5)
            for e in range(E):
                pool.memset(rank_desc[:, :, e:e + 1], float(E - e))
            pool.memset(negmaxT[:, :, :].bitcast(f32), 0.0)
            for k in range(2):
                pool.memset(router_hi0[k][:, 1, :].bitcast(f32), 0.0)
            pool.memset(be_hilo[:, :].bitcast(f32), 0.0).then_inc(consts_ready, 1)

            def low_part(n, part, whole):
                pool.wait_ge(W_hi, n)
                pool.tensor_tensor(part[lo][:, :], whole, part[hi][:, :].bitcast(f32), ALU.subtract).then_inc(W_lo, 1)

            def add_weighted(step):
                _, b, i = step
                j = 2 * (i // 2)
                pool.wait_ge(x_weighted, 2 * x_turn(step))
                pool.tensor_tensor(weighted[:, :, 0:2, :], weighted[:, :, 0:2, :], weighted[:, :, 2:4, :], ALU.add
                                   ).then_inc(x_paired, 1)
                pool.wait_ge(x_paired, 2 * x_turn(step) - 1)
                pool.tensor_tensor(weighted[:, :, 0, :], weighted[:, :, 0, :], weighted[:, :, 1, :], ALU.add
                                   ).then_inc(x_paired, 1)
                pool.wait_ge(x_paired, 2 * x_turn(step))
                pool.wait_ge(x_read, 2 * x_turn(("X", b, i - 1)))
                pool.tensor_tensor(resid[:, b, j:j + 2, :], resid[:, b, j:j + 2, :], weighted[:, :, 0, :], ALU.add
                                   ).then_inc(x2_ready, 1)

            def k_all(b):
                pool.wait_ge(KT_lo, 1)
                pool.wait_ge(masks_ready, 1)
                if b >= 2:
                    pool.wait_ge(e_psum, turn["exp", b - 2, NC4 - 1])
                for part in (hi, lo):
                    pool.tensor_tensor(K_all[part][:, b % 2, :, :],
                                       KT_p[part][:, b, :].bitcast(f32).unsqueeze(1).broadcast_to([P, H, NKEY]),
                                       head_mask[:, :].unsqueeze(2).broadcast_to([P, H, NKEY]), ALU.mult
                                       ).then_inc(K_all_ready, 1)

            for step in steps:
                kind, b, i = step
                n = LNS * b + i
                if kind == "stats":
                    pool.wait_ge(var_ready, turn[step])
                    link(pool.tensor_scalar(var_eps[:, n, :], mean_var[:, n, :, 1], EPS, 1.0, ALU.add, ALU.mult))
                    pool.tensor_tensor(rstd[:, n, :], var_eps[:, n, :], minus_half[:, :], ALU.pow
                                       ).then_inc(rstd_ready, 1)
                if kind == "keys":
                    k_all(b)
                if kind == "Q":
                    pool.wait_ge(xn_dve, turn["norm", b, 0])
                    pool.wait_ge(xn_act, turn["norm", b, 0])
                    pool.wait_ge(ld_o, 32)
                    pool.tensor_tensor(resid[:, b, :, :], resid[:, b, :, :],
                                       bo_all[:, :].unsqueeze(1).broadcast_to([P, J, D]), ALU.add
                                       ).then_inc(xb_ready, 1)
                if kind == "first_weights":
                    pool.memset(gateT[:, :, :].bitcast(f32), 0.0).then_inc(gateT_zeroed, 1)
                    pool.wait_ge(be_ready, 1)
                    pool.wait_ge(W_hi, 2)
                    pool.tensor_tensor(router_hilo[0][:, 1, :], Wg_sb[:, :], router_hilo[0][:, 0, :].bitcast(f32),
                                       ALU.subtract).then_inc(W_lo, 1)
                    pool.tensor_tensor(be_lo, be_sb, be_hilo[0:1, :].bitcast(f32), ALU.subtract
                                       ).then_inc(be_ready, 1)
                    low_part(3, We_p, flat(We_sb[:, :, :]))
                if kind == "second_weights":
                    low_part(4, w1_p, w1_sb[:, :])
                    low_part(5, w3_p, w3_sb[:, :])
                if kind == "third_weights":
                    low_part(6, w2_p, w2_sb[:, :])
                if kind == "X" and i % 2 == 1:
                    add_weighted(step)
                if kind == "rows":
                    pool.wait_ge(rows_in[b], 64)
                    pool.tensor_tensor(flat(resid[:, b, :, :]), flat(resid[:, b, :, :]), memory_rows[:, b, :],
                                       ALU.add).then_inc(x3_ready, 1)
                if kind == "split":
                    n = turn[step]
                    if n == 1:
                        pool.wait_ge(be_moved, 16)
                    pool.wait_ge(hidden_hi, n)
                    pool.tensor_tensor(hidden_p[lo][:, n % 2, :], hidden[:, n % 2, :],
                                       hidden_p[hi][:, n % 2, :].bitcast(f32), ALU.subtract).then_inc(hidden_lo, 1)

        @block.scalar
        def _(act):
            def high_part(part, whole):
                act.activation(part[hi][:, :], whole, ACT.Copy).then_inc(W_hi, 1)

            act.wait_ge(ctxT_psum, 1)
            act.activation(ctxT[:, :, :, :],
                           bank[0][:, 0:B * NKEY].rearrange("p (b k) -> p b k", b=B).unsqueeze(2)
                           .broadcast_to([P, B, H4, NKEY]), ACT.Copy).then_inc(ctxT_ready, 1)

            for step in steps:
                kind, b, i = step
                par = b % 2
                if kind == "first_weights":
                    act.wait_ge(consts_ready, 1)
                    act.activation(ones_r[:, :], ones[:, :], ACT.Copy)
                    act.wait_ge(ld_ffn0, 80)
                    act.activation(be_hilo[0:1, :], be_sb, ACT.Copy).then_inc(be_ready, 1)
                    act.activation(router_hilo[0][:, 0, :], Wg_sb[:, :], ACT.Copy).then_inc(W_hi, 1)
                    act.activation(router_hi0[0][:, 0, :], Wg_sb[:, :], ACT.Copy).then_inc(W_hi, 1)
                    high_part(We_p, flat(We_sb[:, :, :]))
                    act.wait_ge(wr_psum, 1)
                    act.activation(router_hilo[1][:, 0, :], ps_of(step)[:, 0:E], ACT.Copy)
                    act.activation(router_hi0[1][:, 0, :], ps_of(step)[:, 0:E], ACT.Copy).then_inc(wr_hi, 1)
                if kind == "second_weights":
                    act.wait_ge(ld_w13, 32)
                    high_part(w1_p, w1_sb[:, :])
                    high_part(w3_p, w3_sb[:, :])
                if kind == "third_weights":
                    act.wait_ge(ld_w2, 16)
                    high_part(w2_p, w2_sb[:, :])
                if kind == "keys" and b == 0:
                    act.wait_ge(KT_ready, 1)
                    act.activation(KT_p[hi][:, :, :], KT[:, :, :], ACT.Copy).then_inc(KT_hi, 1)
                if kind == "norm":
                    n = LNS * b + i
                    act.wait_ge(shift_ready, turn[step])
                    if xn_read_by(b, i):
                        act.wait_ge(xT_psum, turn[xn_read_by(b, i)])
                    for j in range(NORM_V, J):
                        last = act.activation(xn[:, xn_slot(b, i), j, :], resid[:, b, j, :], ACT.Identity,
                                              bias=neg_mean_rstd[:, n, j:j + 1], scale=rstd[:, n, j:j + 1])
                    last.then_inc(xn_act, 1)
                if kind == "T":
                    act.wait_ge(xT_psum, turn[step])
                    if i == 0 and first_ln_before(b) is not None:
                        act.wait_ge(q_psum, turn["Q", first_ln_before(b), 0])
                    if i == 1 and b >= 2:
                        act.wait_ge(x_psum, turn["X", b - 2, 3])
                    if i == 3 and b >= 3:
                        act.wait_ge(h3_psum, turn["h3", b - 3, NCH - 1])
                    act.activation(x1T[:, :] if i == 0 else split_xT(i, b)[hi], ps_of(step)[:, :], ACT.Copy
                                   ).then_inc(xT_hi, 1)
                if kind == "Q":
                    act.wait_ge(q_psum, turn[step])
                    if b >= 2:
                        act.wait_ge(e_psum, turn["exp", b - 2, NC4 - 1])
                    act.activation(q_p[hi][:, par, :], ps_of(step)[:, :], ACT.Identity, bias=bq_col[:, :]
                                   ).then_inc(q_hi, 1)
                if kind == "maxT":
                    act.wait_ge(nT_psum, turn[step])
                    if b >= 2:
                        act.wait_ge(e_psum, turn["exp", b - 2, NC4 - 1])
                    act.wait_ge(consts_ready, 1)
                    act.activation(negmaxT[0:H, par, :], ps_of(step)[0:H, :], ACT.Copy).then_inc(nT_ready, 1)
                if kind == "exp":
                    act.wait_ge(e_psum, turn[step])
                    if b >= 2:
                        act.wait_ge(pv_psum, turn["V", b - 2, 1])
                    act.activation(probsT[:, par, i, :], ps_of(step)[:, :], ACT.Exp, scale=SCALE
                                   ).then_inc(probs_ready, 1)
                if kind == "attnT":
                    act.wait_ge(aT_psum, turn[step])
                    if b >= 2:
                        act.wait_ge(o_psum, turn["O", b - 2, 0])
                    act.activation(aT[:, par, :], ps_of(step)[:, :], ACT.Copy).then_inc(aT_ready, 1)
                if kind == "route":
                    act.wait_ge(shifted, turn[step])
                    act.activation(rt[par][1][:, :, :], rt[par][0][:, :, :], ACT.Exp).then_inc(exps, 1)
                if kind == "X" and i % 2 == 1:
                    act.wait_ge(x_psum, turn[step])
                    act.wait_ge(gate_ready, turn["weigh", b, 0])
                    if x_turn(step) == 1:
                        act.wait_ge(W_lo, 2)
                    else:
                        act.wait_ge(x2_ready, x_turn(step) - 1)
                    for u in range(2):
                        j = 2 * (i // 2) + u
                        for e in range(E // 2):
                            last = act.activation(weighted[:, u, e, :], ps_of(step, u)[:, D * e:D * e + D], ACT.Copy,
                                                  scale=gate[:, 0, b, j, E // 2 + e:E // 2 + e + 1])
                        last.then_inc(x_weighted, 1)
                if kind == "conv":
                    act.wait_ge(convT_psum, turn[step])
                    if b >= 2:
                        act.wait_ge(comp_psum, turn["conv", b - 2, 0])
                    act.activation(convT[:, par, :, :], ps_of(step)[:, 0:J * COMP], ACT.Copy).then_inc(convT_ready, 1)
                if kind == "gateT":
                    act.wait_ge(gT_psum, turn[step])
                    act.wait_ge(gateT_zeroed, 1)
                    if b >= 3:
                        act.wait_ge(gb_psum, turn["gate", b - 3, NCH - 1])
                    act.activation(gateT[0:2 * E, b % 3, :], ps_of(step)[0:2 * E, :], ACT.Copy).then_inc(gT_ready, 1)
                if kind == "h3":
                    n = turn[step]
                    act.wait_ge(h1_psum, n)
                    if n > 2:
                        act.wait_ge(gated_ready, n - 2)
                    act.activation(silu_h[:, n % 2, :], ps_h1[:, :], ACT.Silu).then_inc(silu_ready, 1)
                if kind == "split":
                    n = turn[step]
                    act.wait_ge(hidden_ready, n)
                    if n > 2:
                        act.wait_ge(y_psum, n - 2)
                    act.activation(hidden_p[hi][:, n % 2, :], hidden[:, n % 2, :], ACT.Copy).then_inc(hidden_hi, 1)
                if kind == "out":
                    act.wait_ge(y_psum, turn["y", b, NCH - 1])
                    act.activation(yT[:, :], ps_y[:, :], ACT.Copy).then_inc(yT_ready, 1)

        @block.vector
        def _(dve):
            own = [0]

            def link(ins):
                own[0] += 1
                ins.then_inc(dve_step, 1)
                dve.wait_ge(dve_step, own[0])

            def masks():
                dve.wait_ge(ident_ready, 1)
                dve.tensor_reduce(head_mask[:, :], ident[:, :].rearrange("p (h k) -> p h k", h=H), AX.X, ALU.add)
                link(dve.tensor_reduce(key_head_mask[:, :], ident[:, :].rearrange("p (h k) -> p h k", h=H4), AX.X,
                                       ALU.add))
                dve.tensor_tensor(expert_mask[:, :], ident[:, 0:E], ident[:, E:2 * E], ALU.add).then_inc(masks_ready, 1)
                dve.wait_ge(masks_ready, 1)

            def keys():
                dve.wait_ge(kv_psum, 1)
                dve.tensor_scalar(KT[:, :, :].rearrange("p b k -> p (b k)"), bank[1][:, 0:B * NKEY], bk_col[:, :], None,
                                  ALU.add).then_inc(KT_ready, 1)
                dve.wait_ge(KT_hi, 1)
                dve.tensor_tensor(KT_p[lo][:, :, :], KT[:, :, :], KT_p[hi][:, :, :].bitcast(f32), ALU.subtract
                                  ).then_inc(KT_lo, 1)

            def values(step):
                dve.tensor_copy(head_rows[:, :, :], ident[:, 0:H].unsqueeze(2).broadcast_to([P, H, NKEY])
                                ).then_inc(rows_ready, 1)
                dve.wait_ge(kv_psum, 2)
                v_ps = ps_of(step)[:, :].rearrange("p (b c h k) -> p b c h k", b=B, c=NC4, h=H4)
                for b in range(B):
                    last = dve.tensor_tensor(V_aug[:, b, :, :, 0:DK], v_ps[:, b],
                                             key_head_mask[:, :].unsqueeze(1).unsqueeze(3).broadcast_to([P, NC4, H4, DK]),
                                             ALU.mult)
                last.then_inc(V_ready, 1)
                dve.tensor_copy(V_aug[:, :, :, :, DK:VW].rearrange("p b c h a -> p (b c) (h a)"),
                                key_head_mask[:, :].unsqueeze(1).broadcast_to([P, B * NC4, H4])).then_inc(V_ready, 1)
                dve.tensor_copy(expert_rows[:, :, :], expert_mask[:, :].unsqueeze(2).broadcast_to([P, E, HID])
                                ).then_inc(rows_ready, 1)

            def route(step):
                kind, b, k = step
                d, ex, l, key, one1, l2, d2, one2, sel = rt[b % 2]
                picked = key
                m1, k1, m2, k2, total, inv = rs[b % 2]

                def bc(v):
                    return v[:, :].unsqueeze(2).broadcast_to([P, J, E])

                if kind == "route":
                    dve.wait_ge(logit_psum, turn[step])
                    if k == 0 and b >= 2:
                        dve.wait_ge(gate_ready, turn["weigh", b - 2, 1])
                    logits = ps_of(step)[:, 0:J * 2 * E].rearrange("p (j s e) -> p j e s", j=J, s=2)
                    dve.tensor_reduce(l[:, :, :], logits, AX.X, ALU.add).then_inc(logit_read, 1)
                    if k == 0:
                        dve.wait_ge(logit_read, turn[step])
                        link(dve.tensor_tensor(l[:, :, :], l[:, :, :],
                                               bg_all[:, :].unsqueeze(1).broadcast_to([P, J, E]), ALU.add))
                    dve.wait_ge(logit_read, turn[step])
                    link(dve.tensor_reduce(m1[:, :], l[:, :, :], AX.X, ALU.max))
                    dve.tensor_tensor(d[:, :, :], l[:, :, :], bc(m1), ALU.subtract).then_inc(shifted, 1)
                    dve.wait_ge(shifted, turn[step])
                    return
                if kind == "pick":
                    link(dve.scalar_tensor_tensor(flat(key[:, :, :]), flat(d[:, :, :]), 0.0, flat(rank_desc[:, :, :]),
                                                  ALU.is_ge, ALU.mult))
                    link(dve.tensor_reduce(k1[:, :], key[:, :, :], AX.X, ALU.max))
                    link(dve.tensor_tensor(one1[:, :, :], key[:, :, :], bc(k1), ALU.is_equal))
                    link(dve.scalar_tensor_tensor(flat(l2[:, :, :]), flat(one1[:, :, :]), -1e38, flat(d[:, :, :]),
                                                  ALU.mult, ALU.add))
                    link(dve.tensor_reduce(m2[:, :], l2[:, :, :], AX.X, ALU.max))
                    return
                link(dve.tensor_tensor(d2[:, :, :], l2[:, :, :], bc(m2), ALU.subtract))
                link(dve.scalar_tensor_tensor(flat(key[:, :, :]), flat(d2[:, :, :]), 0.0, flat(rank_desc[:, :, :]),
                                              ALU.is_ge, ALU.mult))
                link(dve.tensor_reduce(k2[:, :], key[:, :, :], AX.X, ALU.max))
                link(dve.tensor_tensor(one2[:, :, :], key[:, :, :], bc(k2), ALU.is_equal))
                link(dve.tensor_tensor(sel[:, :, :], one1[:, :, :], one2[:, :, :], ALU.add))
                dve.wait_ge(exps, turn["route", b, k])
                link(dve.tensor_tensor(picked[:, :, :], ex[:, :, :], sel[:, :, :], ALU.mult))
                link(dve.tensor_reduce(total[:, :], (picked if k == 0 else ex)[:, :, :], AX.X, ALU.add))
                link(dve.reciprocal(inv[:, :], total[:, :]))
                weights = gate[:, k, b, :, :]
                last = dve.tensor_tensor(weights, picked[:, :, :], bc(inv), ALU.mult)
                if k == 1:
                    link(last)
                    parts = gate_hilo[:, b, :, :]
                    link(dve.tensor_copy(parts[:, :, 0:E], weights))
                    last = dve.tensor_tensor(parts[:, :, E:2 * E], weights, parts[:, :, 0:E].bitcast(f32),
                                             ALU.subtract)
                last.then_inc(gate_ready, 1)
                dve.wait_ge(gate_ready, turn[step])

            for step in steps:
                kind, b, i = step
                par = b % 2
                if step == ("norm", 0, 0):
                    masks()
                if kind == "keys" and b == 0:
                    keys()
                if kind == "values":
                    values(step)
                if kind == "first_weights":
                    dve.wait_ge(wr_hi, 1)
                    dve.tensor_tensor(router_hilo[1][:, 1, :], ps_of(step)[:, 0:E],
                                      router_hi0[1][:, 0, :].bitcast(f32), ALU.subtract).then_inc(wr_lo, 1)
                if kind == "stats":
                    n = LNS * b + i
                    if i == 0:
                        dve.wait_ge(ld_x[b], 16)
                    if i == 1:
                        dve.wait_ge(x1_ready, turn["O", b, 0])
                    if i == 2:
                        dve.wait_ge(x2_ready, x_turn(("X", b, 3)))
                    if i == 3:
                        dve.wait_ge(x3_ready, turn["rows", b, 0])
                    for j in range(J):
                        last = dve.bn_stats(bn[:, n, j, :], resid[:, b, j, :])
                    link(last)
                    for j in range(J):
                        last = dve.bn_aggr(mean_var[:, n, j, :], bn[:, n, j, :])
                    last.then_inc(var_ready, 1)
                if kind == "norm":
                    n = LNS * b + i
                    dve.wait_ge(rstd_ready, turn["stats", b, i])
                    dve.scalar_tensor_tensor(neg_mean_rstd[:, n, NORM_V:J], mean_var[:, n, NORM_V:J, 0], -1.0,
                                             rstd[:, n, NORM_V:J], ALU.mult, ALU.mult).then_inc(shift_ready, 1)
                    if xn_read_by(b, i):
                        dve.wait_ge(xT_psum, turn[xn_read_by(b, i)])
                    for j in range(NORM_V):
                        last = dve.tensor_scalar(xn[:, xn_slot(b, i), j, :], resid[:, b, j, :], mean_var[:, n, j, 0:1],
                                                 rstd[:, n, j:j + 1], ALU.subtract, ALU.mult)
                    last.then_inc(xn_dve, 1)
                if kind == "T" and i > 0:
                    dve.wait_ge(xT_hi, turn[step])
                    dve.tensor_tensor(split_xT(i, b)[lo], ps_of(step)[:, :], split_xT(i, b)[hi].bitcast(f32),
                                      ALU.subtract).then_inc(xT_lo, 1)
                if kind == "Q":
                    dve.wait_ge(q_hi, turn[step])
                    dve.scalar_tensor_tensor(q_p[lo][:, par, :], ps_of(step)[:, :], bq_col[:, :],
                                             q_p[hi][:, par, :].bitcast(f32), ALU.add, ALU.subtract).then_inc(q_lo, 1)
                if kind == "max":
                    dve.wait_ge(m_psum, turn[step])
                    if b >= 2:
                        dve.wait_ge(nT_psum, turn["maxT", b - 2, 0])
                    dve.tensor_reduce(negmax[:, par, i, :], ps_of(step)[:, :].rearrange("p (h k) -> p h k", h=H),
                                      AX.X, ALU.max, negate=True).then_inc(negmax_ready, 1)
                if kind == "V":
                    ps = ps_of(step)[:, 0:2 * H * VW].rearrange("p (h v) -> p h v", v=VW)
                    dve.wait_ge(pv_psum, turn[step])
                    if b >= 2:
                        dve.wait_ge(aT_psum, turn["attnT", b - 2, 0])
                    link(dve.reciprocal(rden[:, 2 * par + i, :], ps[:, :, DK]))
                    dve.tensor_tensor(attn[:, par, 2 * i:2 * i + 2, :, :].rearrange("p j h k -> p (j h) k"),
                                      ps[:, :, 0:DK], rden[:, 2 * par + i, :].unsqueeze(2).broadcast_to([P, 2 * H, DK]),
                                      ALU.mult).then_inc(attn_ready, 1)
                if kind == "O":
                    dve.wait_ge(o_psum, turn[step])
                    dve.wait_ge(xb_ready, turn["Q", b, 0])
                    dve.tensor_tensor(flat(resid[:, b, :, :]), ps_of(step)[:, :], flat(resid[:, b, :, :]), ALU.add
                                      ).then_inc(x1_ready, 1)
                if kind in ("route", "pick", "weigh"):
                    if step == ("route", 0, 0):
                        dve.wait_ge(ld_ffn0, 80)
                        dve.wait_ge(consts_ready, 1)
                    route(step)
                if kind == "X" and i % 2 == 0:
                    dve.wait_ge(x_psum, turn[step])
                    jj = i // 2
                    for e in range(E // 2):
                        for u in range(2):
                            j = 2 * jj + u
                            ins = dve.scalar_tensor_tensor(resid[:, b, j, :], ps_of(step, u)[:, D * e:D * e + D],
                                                           gate[:, 0, b, j, e:e + 1],
                                                           resid[:, b, j, :], ALU.mult, ALU.add)
                            if e == E // 2 - 1:
                                ins.then_inc(x_read, 1)
                            else:
                                own[0] += 1
                                ins.then_inc(dve_step, 1)
                            if not (e == E // 2 - 1 and u == 1):
                                if e or u:
                                    dve.wait_ge(dve_step, own[0] - (1 if e < E // 2 - 1 else 0))
                    dve.wait_ge(x_read, 2 * x_turn(step))
                if kind == "conv":
                    dve.wait_ge(comp_psum, turn[step])
                    if b < 2:
                        dve.wait_ge(ld_conv, 32)
                    else:
                        dve.wait_ge(rows_in[b - 2], 64)
                    dve.tensor_tensor(comp[:, par, :], ps_of(step, 1)[0:COMP, 0:D], convb_all[:, :], ALU.add
                                      ).then_inc(comp_ready, 1)
                if kind == "gate":
                    n = turn[step]
                    dve.wait_ge(silu_ready, n)
                    dve.wait_ge(h3_psum, n)
                    if n > 2:
                        dve.wait_ge(hidden_ready, n - 2)
                    dve.tensor_tensor(gated[:, n % 2, :], ps_h3[n % 2][:, :], silu_h[:, n % 2, :], ALU.mult
                                      ).then_inc(gated_ready, 1)
                    dve.wait_ge(gated_ready, n)
                    dve.wait_ge(gb_psum, n)
                    if n == 1:
                        dve.wait_ge(be_ready, 2)
                    if n > 2:
                        dve.wait_ge(hidden_lo, n - 2)
                    dve.tensor_tensor(hidden[:, n % 2, :], ps_gate[:, :], gated[:, n % 2, :], ALU.mult
                                      ).then_inc(hidden_ready, 1)
                if kind == "out":
                    dve.wait_ge(yt_psum, b + 1)
                    dve.tensor_tensor(flat(resid[:, b, :, :]), ps_of(step)[:, :], flat(resid[:, b, :, :]), ALU.add
                                      ).then_inc(x4_ready, 1)

        @block.tensor
        def _(pe):
            last_reader = {}

            def take(step, reader, count, i=0):
                k = bank_of[(*step, i)]
                if k in last_reader:
                    pe.wait_ge(*last_reader[k])
                last_reader[k] = (reader, count)
                return bank[k]

            def take_over(k):
                if k in last_reader:
                    pe.wait_ge(*last_reader.pop(k))

            def three_passes(o, lhs, rhs, start=True, stop=True):
                pe.matmul(o, lhs[hi], rhs[hi], start=start, stop=False)
                pe.matmul(o, lhs[lo], rhs[hi], start=False, stop=False)
                return pe.matmul(o, lhs[hi], rhs[lo], start=False, stop=stop)

            pe.wait_ge(ident_ready, 1)
            pe.wait_ge(ld_ctx, 48)
            ps = take(("setup", 0, 0), ctxT_ready, 1, 0)
            pe.transpose(ps[:, 0:P], ctx_sb[:, :], ident[:, :]).then_inc(ctxT_psum, 1)
            pe.wait_ge(ctxT_ready, 1)
            ps = take(("setup", 0, 0), KT_ready, 1, 1)
            pe.matmul(ps[:, 0:P], Wk_sb[:, :], ctxT[:, :, 0, :], start=True, stop=True).then_inc(kv_psum, 1)

            for step in steps:
                kind, b, i = step
                par = b % 2
                n = turn[step]
                if kind == "values":
                    ps = take(step, V_ready, 2)
                    pe.wait_ge(ld_v, 32)
                    for b in range(B):
                        pe.matmul(ps[:, D * b:D * b + D], ctxT[:, b, :, :].rearrange("p h k -> p (h k)"), Wv_sb[:, :],
                                  start=True, stop=False)
                        last = pe.matmul(ps[:, D * b:D * b + D], ones[:, :], bv_row[:, :], start=False, stop=True)
                    last.then_inc(kv_psum, 1)
                if kind == "T":
                    ps = take(step, xT_hi if i == 0 else xT_lo,
                              n if i == 0 else xT_splits(b, i))
                    pe.wait_ge(xn_dve, turn["norm", b, i])
                    pe.wait_ge(xn_act, turn["norm", b, i])
                    for j in range(J):
                        last = pe.transpose(ps[:, P * j:P * j + P], xn[:, xn_slot(b, i), j, :], ident[:, :])
                    last.then_inc(xT_psum, 1)
                if kind == "first_weights":
                    ps = take(step, wr_lo, 1)
                    pe.wait_ge(ld_ffn0, 80)
                    pe.transpose(ps[:, 0:E], wr_sb[:, :], ident[0:E, 0:E]).then_inc(wr_psum, 1)
                if kind == "Q":
                    ps = take(step, q_lo, n)
                    pe.wait_ge(ld_q, 32)
                    pe.wait_ge(xT_hi, turn["T", b, 0])
                    pe.matmul(ps[:, :], Wq_sb[:, :], x1T[:, :], start=True, stop=True).then_inc(q_psum, 1)
                if kind == "max":
                    ps = take(step, negmax_ready, n)
                    pe.wait_ge(q_hi, turn["Q", b, 0])
                    pe.wait_ge(K_all_ready, 2 * turn["keys", b, 0])
                    pe.matmul(ps[:, :], q_p[hi][:, par, P * i:P * i + P], flat(K_all[hi][:, par, :, :]),
                              start=True, stop=True).then_inc(m_psum, 1)
                if kind == "maxT":
                    ps = take(step, nT_ready, n)
                    pe.wait_ge(negmax_ready, turn["max", b, J - 1])
                    for j in range(J):
                        last = pe.transpose(ps[0:H, P * j:P * j + P], negmax[:, par, j, :], ident[:, :])
                    last.then_inc(nT_psum, 1)
                if kind == "exp":
                    ps = take(step, probs_ready, n)
                    pe.wait_ge(nT_ready, turn["maxT", b, 0])
                    pe.wait_ge(rows_ready, 1)
                    pe.wait_ge(q_lo, turn["Q", b, 0])
                    three_passes(ps[:, :], [flat(w[:, par, H4 * i:H4 * i + H4, :]) for w in K_all],
                                 [q[:, par, :] for q in q_p], stop=False)
                    pe.matmul(ps[:, :], flat(head_rows[:, H4 * i:H4 * i + H4, :]), negmaxT[:, par, :],
                              start=False, stop=True).then_inc(e_psum, 1)
                if kind == "V":
                    ps = take(step, attn_ready, n)
                    pe.wait_ge(probs_ready, turn["exp", b, NC4 - 1])
                    pe.wait_ge(V_ready, 2)
                    for u in range(2):
                        j = 2 * i + u
                        for c in range(NC4):
                            at = u * H * VW + c * H4 * VW
                            last = pe.matmul(ps[:, at:at + H4 * VW], probsT[:, par, c, P * j:P * j + P],
                                             flat(V_aug[:, b, c, :, :]), start=True, stop=True)
                    last.then_inc(pv_psum, 1)
                if kind == "attnT":
                    ps = take(step, aT_ready, n)
                    pe.wait_ge(attn_ready, turn["V", b, 1])
                    for j in range(J):
                        last = pe.transpose(ps[:, P * j:P * j + P], flat(attn[:, par, j, :, :]), ident[:, :])
                    last.then_inc(aT_psum, 1)
                if kind == "O":
                    ps = take(step, x1_ready, n)
                    pe.wait_ge(aT_ready, turn["attnT", b, 0])
                    pe.wait_ge(ld_o, 32)
                    for j in range(J):
                        last = pe.matmul(ps[:, D * j:D * j + D], aT[:, par, P * j:P * j + P], Wo_sb[:, :],
                                         start=True, stop=True)
                    last.then_inc(o_psum, 1)
                if kind == "route":
                    ln = 1 if i == 0 else 3
                    ps = take(step, logit_read, n)
                    pe.wait_ge(xT_lo, xT_splits(b, ln))
                    if i == 0:
                        pe.wait_ge(W_lo, 1)
                    else:
                        pe.wait_ge(wr_lo, 1)
                    for u in range(J):
                        x_hi, x_lo = [a[:, P * u:P * u + P] for a in split_xT(ln, b)]
                        o = ps[:, 2 * E * u:2 * E * u + 2 * E]
                        pe.matmul(o, x_hi, flat(router_hilo[i][:, :, :]), start=True, stop=False)
                        last = pe.matmul(o, x_lo, flat(router_hi0[i][:, :, :]), start=False, stop=True)
                    last.then_inc(logit_psum, 1)
                if kind == "X":
                    cols = slice(D * E // 2 * (i % 2), D * E // 2 * (i % 2 + 1))
                    pe.wait_ge(W_lo, 2)
                    pe.wait_ge(be_moved, 16)
                    for u in range(2):
                        j = 2 * (i // 2) + u
                        ps = take(step, x_weighted if i % 2 else x_read, 2 * (x_turn(step) - 1) + u + 1, u)
                        three_passes(ps[:, :], [a[:, P * j:P * j + P] for a in split_xT(1, b)],
                                     [w[:, cols] for w in We_p], stop=False)
                        last = pe.matmul(ps[:, :], ones_r[:, :], be_hilo[:, cols], start=False, stop=True)
                    last.then_inc(x_psum, 1)
                if kind == "conv":
                    ps = take(step, convT_ready, n)
                    pe.wait_ge(xn_dve, turn["norm", b, 2])
                    pe.wait_ge(xn_act, turn["norm", b, 2])
                    at = HALF // J
                    for j in range(J):
                        last = pe.transpose(ps[:, COMP * j:COMP * j + COMP], xn[at:at + COMP, par, j, :],
                                            ident[at:at + COMP, at:at + COMP])
                    last.then_inc(convT_psum, 1)
                    ps = take(step, comp_ready, n, 1)
                    pe.wait_ge(convT_ready, n)
                    pe.wait_ge(ld_conv, 32)
                    for j in range(J):
                        last = pe.matmul(ps[0:COMP, 0:D], convT[:, par, j, :], conv_sb[:, j, :],
                                         start=(j == 0), stop=(j == J - 1))
                    last.then_inc(comp_psum, 1)
                if kind == "gateT":
                    ps = take(step, gT_ready, n)
                    pe.wait_ge(gate_ready, turn["weigh", b, 1])
                    for j in range(J):
                        last = pe.transpose(ps[0:2 * E, P * j:P * j + P], gate_hilo[:, b, j, :].bitcast(f32), ident[:, :])
                    last.then_inc(gT_psum, 1)
                cols = slice(P * i, P * i + P)
                if kind == "h1":
                    if n == 1:
                        take_over(H1_BANK)
                    pe.wait_ge(W_lo, 4)
                    pe.wait_ge(xT_lo, xT_splits(b, 3))
                    if n > 1:
                        pe.wait_ge(silu_ready, n - 1)
                    three_passes(ps_h1[:, :], [w[:, cols] for w in w1_p], split_xT(3, b)).then_inc(h1_psum, 1)
                if kind == "h3":
                    if n <= 2:
                        take_over(H3_BANKS[n % 2])
                    if n > 2:
                        pe.wait_ge(gated_ready, n - 2)
                    three_passes(ps_h3[n % 2][:, :], [w[:, cols] for w in w3_p], split_xT(3, b)).then_inc(h3_psum, 1)
                if kind == "gate":
                    if n == 1:
                        take_over(GATE_BANK)
                    pe.wait_ge(gT_ready, turn["gateT", b, 0])
                    pe.wait_ge(rows_ready, 2)
                    if n > 1:
                        pe.wait_ge(hidden_ready, n - 1)
                    pe.matmul(ps_gate[:, :], flat(expert_rows[:, :, :])[:, cols], gateT[:, b % 3, :],
                              start=True, stop=True).then_inc(gb_psum, 1)
                if kind == "y":
                    if n == 1:
                        take_over(Y_BANK)
                    pe.wait_ge(W_lo, 5)
                    pe.wait_ge(hidden_lo, n)
                    if i == 0 and b >= 1:
                        pe.wait_ge(yT_ready, b)
                    three_passes(ps_y[:, :], [w[:, cols] for w in w2_p], [a[:, n % 2, :] for a in hidden_p],
                                 start=(i == 0), stop=(i == NCH - 1)).then_inc(y_psum, 1)
                if kind == "out":
                    pe.wait_ge(yT_ready, b + 1)
                    ps = take(step, x4_ready, b + 1)
                    for j in range(J):
                        last = pe.transpose(ps[:, P * j:P * j + P], yT[:, P * j:P * j + P], ident[:, :])
                    last.then_inc(yt_psum, 1)


_INS = ['x', 'ctx_1024', 'L0_xattn_Wq', 'L0_xattn_bq', 'L0_xattn_Wk', 'L0_xattn_bk', 'L0_xattn_Wv', 'L0_xattn_bv',
        'L0_xattn_Wo', 'L0_xattn_bo', 'L0_ffn_We', 'L0_ffn_be', 'L0_ffn_Wg', 'L0_ffn_bg', 'L1_xattn_conv_w',
        'L1_xattn_conv_b', 'L1_ffn_w_router', 'L1_ffn_w1', 'L1_ffn_w2', 'L1_ffn_w3']
_OUTS = [((4, 512, 128), 'float32')]


def kernel(**inputs):
    import numpy as _np
    import concourse.bacc as _bacc
    from concourse import mybir as _mybir
    from concourse.bass_utils import run_bass_kernel_spmd as _run

    nc = _bacc.Bacc("TRN2", target_bir_lowering=False, num_devices=1)
    arrays, args = {}, []
    for name in _INS:
        a = _np.ascontiguousarray(inputs[name])
        arrays[f"in_{name}_dram"] = a
        args.append(nc.dram_tensor(f"in_{name}_dram", a.shape, _mybir.dt.from_np(a.dtype), kind="ExternalInput").ap())
    for i, (shape, dtype) in enumerate(_OUTS):
        dt = _mybir.dt.from_np(_np.dtype(dtype))
        args.append(nc.dram_tensor(f"out_{i}_dram", shape, dt, kind="ExternalOutput").ap())
    block_program(nc, *args)
    r = _run(nc, [arrays], core_ids=[0])
    got = tuple(r.results[0][f"out_{i}_dram"] for i in range(len(_OUTS)))
    return got[0]
```
